# Optimizing a Trainium2 kernel written in Bass

```python
import numpy as np
import jax
import jax.numpy as jnp

def _softmax(x, axis=-1):
    return jax.nn.softmax(x, axis=axis)

def _gelu(x):
    return jax.nn.gelu(x, approximate=True)

def _silu(x):
    return jax.nn.silu(x)

def _sigmoid(x):
    return jax.nn.sigmoid(x)

def _layernorm(x, axis=-1, eps=1e-05):
    m = jnp.mean(x, axis=axis, keepdims=True)
    v = jnp.var(x, axis=axis, keepdims=True)
    return (x - m) / jnp.sqrt(v + eps)

def _scatter_add(tgt, idx, src, axis=0):
    return tgt.at[idx].add(src)

def _segment_sum(src, seg, n):
    return jax.ops.segment_sum(src, seg, n)
kernel_name = 'mk_prb_d1_jaxref_r8_709e4a'

def setup_inputs(seed: int=0):
    np.random.seed(seed)
    _w = jnp.asarray

    def _L0_attn_setup():
        import jax, jax.numpy as jnp
        import numpy as np
        B, S, D = (4, 256, 256)
        H, HD = (16, 128)
        key = jax.random.key(seed)
        ks = jax.random.split(key, 5)
        sd = 1.0 / np.sqrt(D)
        return {'hidden_states': jax.random.normal(ks[0], (B, S, D), dtype=jnp.float32), 'Wq': jax.random.uniform(ks[1], (D, H * HD), jnp.float32, -sd, sd), 'Wk': jax.random.uniform(ks[2], (D, H * HD), jnp.float32, -sd, sd), 'Wv': jax.random.uniform(ks[3], (D, H * HD), jnp.float32, -sd, sd), 'Wo': jax.random.uniform(ks[4], (H * HD, D), jnp.float32, -sd, sd)}
    _L0_attn_in = _L0_attn_setup()

    def _L0_ffn_setup():
        import jax, jax.numpy as jnp
        import numpy as np
        HID = 256
        INTER = 1024
        NEXP = 8
        TOPK = 2
        EPS = 1e-05

        def _mock_fused_moe(x, selected_experts, routing_weights, expert_weight):
            y = jnp.einsum('bsh,hd->bsd', x, expert_weight)
            scale = routing_weights.sum(axis=-1, keepdims=True)
            return y * scale
        key = jax.random.key(seed)
        ks = jax.random.split(key, 6)
        s = lambda fan_in: 1.0 / np.sqrt(fan_in)
        return {'hidden_states': jax.random.normal(ks[0], (4, 512, HID), dtype=jnp.float32), 'gate_w': jax.random.uniform(ks[1], (HID, NEXP), jnp.float32, -s(HID), s(HID)), 'up_w': jax.random.uniform(ks[2], (HID, INTER), jnp.float32, -s(HID), s(HID)), 'down_w': jax.random.uniform(ks[3], (INTER, HID), jnp.float32, -s(INTER), s(INTER)), 'expert_weight': jax.random.normal(ks[4], (HID, HID), dtype=jnp.float32), 'ln_gamma': jnp.ones((HID,), jnp.float32), 'ln_beta': jnp.zeros((HID,), jnp.float32)}
    _L0_ffn_in = _L0_ffn_setup()
    _d = {'L0_attn_hidden_states': _L0_attn_in['hidden_states'], 'L0_attn_Wq': _L0_attn_in['Wq'], 'L0_attn_Wk': _L0_attn_in['Wk'], 'L0_attn_Wv': _L0_attn_in['Wv'], 'L0_attn_Wo': _L0_attn_in['Wo'], 'L0_ffn_gate_w': _L0_ffn_in['gate_w'], 'L0_ffn_up_w': _L0_ffn_in['up_w'], 'L0_ffn_down_w': _L0_ffn_in['down_w'], 'L0_ffn_expert_weight': _L0_ffn_in['expert_weight'], 'L0_ffn_ln_gamma': _L0_ffn_in['ln_gamma'], 'L0_ffn_ln_beta': _L0_ffn_in['ln_beta']}
    _x0 = _d['L0_attn_hidden_states']
    _d['L0_attn_hidden_states'] = jax.random.normal(jax.random.fold_in(jax.random.key(seed), 1), (4, 1024, 256), dtype=_x0.dtype)
    del _x0
    return _d

def reference(L0_attn_hidden_states, L0_attn_Wq, L0_attn_Wk, L0_attn_Wv, L0_attn_Wo, L0_ffn_gate_w, L0_ffn_up_w, L0_ffn_down_w, L0_ffn_expert_weight, L0_ffn_ln_gamma, L0_ffn_ln_beta):

    def _L0_attn_ref(hidden_states, Wq, Wk, Wv, Wo):
        import jax, jax.numpy as jnp
        import numpy as np
        B, S, D = (4, 256, 256)
        H, HD = (16, 128)
        b, s, _ = hidden_states.shape
        q = (hidden_states @ Wq).reshape(b, s, H, HD).transpose(0, 2, 1, 3)
        k = (hidden_states @ Wk).reshape(b, s, H, HD).transpose(0, 2, 1, 3)
        v = (hidden_states @ Wv).reshape(b, s, H, HD).transpose(0, 2, 1, 3)
        scale = HD ** (-0.5)
        scores = jnp.einsum('bhqd,bhkd->bhqk', q, k) * scale
        causal = jnp.tril(jnp.ones((s, s), dtype=bool))
        scores = jnp.where(causal, scores, jnp.float32(-jnp.inf))
        probs = jax.nn.softmax(scores, axis=-1)
        out = jnp.einsum('bhqk,bhkd->bhqd', probs, v)
        out = out.transpose(0, 2, 1, 3).reshape(b, s, H * HD)
        return out @ Wo

    def _L0_ffn_ref(hidden_states, gate_w, up_w, down_w, expert_weight, ln_gamma, ln_beta):
        import jax, jax.numpy as jnp
        import numpy as np
        HID = 256
        INTER = 1024
        NEXP = 8
        TOPK = 2
        EPS = 1e-05

        def _mock_fused_moe(x, selected_experts, routing_weights, expert_weight):
            y = jnp.einsum('bsh,hd->bsd', x, expert_weight)
            scale = routing_weights.sum(axis=-1, keepdims=True)
            return y * scale
        residuals = hidden_states
        logits = jnp.einsum('bsh,he->bse', hidden_states, gate_w)
        routing_weights, selected_experts = jax.lax.top_k(logits, TOPK)
        h = jnp.einsum('bsh,hi->bsi', residuals, up_w)
        h = jnp.square(jax.nn.relu(h))
        shared_out = jnp.einsum('bsi,ih->bsh', h, down_w)
        moe_out = _mock_fused_moe(hidden_states, selected_experts, routing_weights, expert_weight)
        y = shared_out + moe_out
        mu = y.mean(axis=-1, keepdims=True)
        var = jnp.mean(jnp.square(y - mu), axis=-1, keepdims=True)
        return (y - mu) * jax.lax.rsqrt(var + EPS) * ln_gamma + ln_beta
    x = L0_attn_hidden_states
    xn = _layernorm(x, axis=-1)
    x = x + _L0_attn_ref(xn, L0_attn_Wq, L0_attn_Wk, L0_attn_Wv, L0_attn_Wo) + _L0_ffn_ref(xn, L0_ffn_gate_w, L0_ffn_up_w, L0_ffn_down_w, L0_ffn_expert_weight, L0_ffn_ln_gamma, L0_ffn_ln_beta)
    return x

_drawn_inputs = setup_inputs


def setup_inputs(seed=0):
    import zlib

    import numpy as np

    out = dict(_drawn_inputs(seed))
    spreads = {'L0_ffn_ln_gamma': (1.0, 0.2), 'L0_ffn_ln_beta': (0.0, 0.1)}
    factors = {}
    for name, (base, spread) in spreads.items():
        noise = np.random.default_rng([zlib.crc32(name.encode()), seed]).standard_normal(out[name].shape)
        drawn = base * np.exp(spread * noise) if base else spread * noise
        out[name] = jnp.asarray(drawn.astype(out[name].dtype))
    for name, factor in factors.items():
        out[name] = (out[name] * factor).astype(out[name].dtype)
    return out
```

```python
from contextlib import ExitStack

import concourse.bass as bass
from concourse import mybir

F32 = mybir.dt.float32
F32R = mybir.dt.float32r
BF16 = mybir.dt.bfloat16
I32 = mybir.dt.int32
ALU = mybir.AluOpType
ACT = mybir.ActivationFunctionType
AX = mybir.AxisListType

P = 128
EPS = 1e-5
MASKED = -1e30
RSQRT_GUESS = float(0x5F3759DF)
NEWTON = 3

TILES = 16
SLOTS = 24
UNITS = 12
HALVES = 4
WO_UNITS = 8
PARTS = 4
SLOT_BEGIN = [0, 4, 12, 16, 24]
PART_QK0, PART_QK1, PART_V, PART_O = range(4)


PROJ_BANK, SPARE0, SPARE1 = range(3)


def step_order(last):
    scores = {0: [4], 1: [5], 2: [6, 7], 4: [8], 5: [9], 6: [10], 8: [11],
              12: [12], 13: [13], 14: [14, 15], 16: [16], 17: [17], 18: [18], 19: [19]}
    weights = {0: PART_QK0, 3: PART_O, 6: PART_QK1, 9: PART_V}
    units = {3: [("proj", 0, PROJ_BANK), ("proj", 1, SPARE0)], 4: [("proj", 2, SPARE1)],
             7: [("wo", 0, PROJ_BANK)], 9: [("wo", 1, SPARE0)], 10: [("proj", 3, SPARE1)],
             13: [("wo", 2, PROJ_BANK)], 14: [("wo", 3, PROJ_BANK)],
             15: [("proj", 4, PROJ_BANK), ("proj", 5, SPARE0)], 16: [("proj", 6, SPARE1)],
             18: [("wo", 4, PROJ_BANK)], 20: [("wo", 5, SPARE0)],
             21: [("proj", 7, SPARE1)], 22: [("proj", 8, PROJ_BANK)], 23: [("proj", 9, SPARE1)]}
    order = [("turn", 0, None)]
    for s in range(SLOTS):
        first, end = s in SLOT_BEGIN, s + 1 in SLOT_BEGIN
        now = [q for q in scores.get(s, []) if not (last and q >= TILES)]
        order += [("scores", q, None) for q in now]
        order += [u for u in units.get(s, []) if not (last and u[0] == "proj")]
        if first:
            order.append(("turn", s + 1, None))
        if s + 2 not in SLOT_BEGIN and s + 1 < SLOTS:
            order.append(("turn", s + 1 if end else s + 2, None))
        order += [("exp", q, None) for q in now]
        if s in weights and not (last and weights[s] != PART_O):
            order.append(("weights", weights[s], None))
        order.append(("pv", s, None))
        if end:
            order.append(("out", SLOT_BEGIN.index(s + 1) - 1, None))
    if not last:
        order += [("proj", 10, PROJ_BANK), ("proj", 11, SPARE0)]
    return order + [("wo", 6, SPARE1), ("wo", 7, PROJ_BANK)]


FIRST_ORDER = [("scores", 0), ("exp", 0), ("proj", 8), ("scores", 1), ("exp", 1), ("proj", 9),
               ("scores", 2), ("exp", 2), ("proj", 10), ("scores", 3), ("exp", 3), ("proj", 11)]


def layer_kernel(nc, x, wq, wk, wv, wo, gate_w, up_w, down_w, expert_w, gamma, beta, out):
    B, S, D = x.shape
    HEADS_D = wq.shape[1]
    INTER = up_w.shape[1]
    EXPERTS = gate_w.shape[1]
    KT = D // P
    NT = S // P
    CH = 512
    NC = S // CH
    TPC = CH // P
    IT = INTER // P
    PAIRS = HEADS_D // (2 * P)
    SCALE = float(P) ** -0.5
    GW = D + EXPERTS
    assert (D, S, KT, NT, NC, IT) == (256, 1024, 2, 8, 2, 8)

    x_v = x.rearrange("b (t p) d -> b p t d", p=P)
    out_v = out.rearrange("b (t p) d -> b p t d", p=P)
    wq_v = wq.rearrange("(k p) (g s c) -> g s p k c", p=P, s=2, c=P)
    wk_v = wk.rearrange("(k p) (g s c) -> g s p k c", p=P, s=2, c=P)
    wv_v = wv.rearrange("(k p) (g c) -> g p k c", p=P, c=2 * P)
    wo_v = wo.rearrange("(g s p) n -> g p s n", p=P, s=2)

    with ExitStack() as ctx:
        def sb(name, shape, dt=F32):
            return ctx.enter_context(nc.sbuf_tensor(name, shape, dt))

        def bank(name, n=1):
            return ctx.enter_context(nc.psum_tensor(name, [P, 512 * n], F32))

        def sem(name):
            return ctx.enter_context(nc.semaphore(name))

        xT_hi, xT_lo = (sb(f"xT_{h}", [P, KT, S], F32R) for h in ("hi", "lo"))
        shared = sb("shared", [P, 16384], F32R)
        qk_hi = shared[:, 0:4096].rearrange("p (h m s) -> p h m s", h=2, m=2)
        qk_lo = shared[:, 4096:8192].rearrange("p (h m s) -> p h m s", h=2, m=2)
        v_hi = shared[:, 8192:10240].rearrange("p (t h c) -> p t h c", t=NT, h=2)
        v_lo = shared[:, 10240:12288].rearrange("p (t h c) -> p t h c", t=NT, h=2)
        oT_hi = shared[:, 12288:14336].rearrange("p (h s) -> p h s", h=2)
        oT_lo = shared[:, 14336:16384].rearrange("p (h s) -> p h s", h=2)
        hid_hi = [shared[:, 8192 * c:8192 * c + 4096].rearrange("p (i s) -> p i s", i=IT) for c in range(NC)]
        hid_lo = [shared[:, 8192 * c + 4096:8192 * c + 8192].rearrange("p (i s) -> p i s", i=IT) for c in range(NC)]
        prob = [sb("prob0", [P, TPC, CH]), sb("prob1", [P, TPC, S])]
        xn = prob[0][:, :, :].rearrange("p r (a d) -> p (r a) d", a=2)
        hid = prob[1][:, :, :].rearrange("p r (a s) -> p (r a) s", a=2)
        pT_hi, pT_lo = (sb(f"pT_{h}", [P, 3, CH], F32R) for h in ("hi", "lo"))
        pD_hi, pD_lo = (sb(f"pD_{h}", [P, 2 * P], F32R) for h in ("hi", "lo"))
        w_raw = sb("w_raw", [P, PARTS, 512])
        w_hi, w_lo = (sb(f"w_{h}", [P, PARTS, 512], F32R) for h in ("hi", "lo"))
        up_hi, up_lo = (sb(f"up_{h}", [P, KT, INTER], F32R) for h in ("hi", "lo"))
        down_hi, down_lo = (sb(f"down_{h}", [P, IT, D], F32R) for h in ("hi", "lo"))
        eg_hi, eg_lo = (sb(f"eg_{h}", [P, KT, GW], F32R) for h in ("hi", "lo"))
        up_raw = prob[1][:, 0:2, :]
        down_raw = prob[1][:, 2:4, :].rearrange("p r (a n) -> p (r a) n", n=D)
        acc = sb("acc", [P, NT, D])
        eg_raw = acc[:, :, :].rearrange("p t d -> p (t d)")[:, 0:KT * GW].rearrange("p (k n) -> p k n", k=KT)
        xin = sb("xin", [P, NT, D])
        y = sb("y", [P, NT, D])
        gamma_b, beta_b = sb("gamma_b", [P, D]), sb("beta_b", [P, D])
        ident = sb("ident", [P, P])
        ident_bf, mask_bf = sb("ident_bf", [P, P], BF16), sb("mask_bf", [P, P], BF16)
        stats = sb("stats", [P, NT, 6])
        mean, var, rstd, tmp, half = (sb(n, [P, NT]) for n in ("mean", "var", "rstd", "tmp", "half"))
        top8 = sb("top8", [P, NT, 8])
        top2 = sb("top2", [P, NT])
        neg_max, prob_sum, prob_rcp = (sb(n, [P, TILES]) for n in ("neg_max", "prob_sum", "prob_rcp"))

        ps_scores = [bank("ps_scores0", 2), bank("ps_scores1", 2)]
        ps_turn = [bank("ps_turn0"), bank("ps_turn1")]
        ps_out, ps_proj = bank("ps_out"), bank("ps_proj")
        banks = [ps_scores[0][:, 0:512], ps_scores[0][:, 512:1024], ps_scores[1][:, 0:512],
                 ps_scores[1][:, 512:1024], ps_turn[0][:, :], ps_turn[1][:, :], ps_out[:, :], ps_proj[:, :]]

        unit_banks = [banks[7], banks[1], banks[3]]

        s_const = sem("constants_made")
        s_fraw = sem("ffn_weights_loaded")
        s_fhi, s_flo = sem("ffn_weights_hi"), sem("ffn_weights_lo")
        s_xin = sem("x_loaded")
        s_raw = [sem(f"weights_loaded{p}") for p in range(PARTS)]
        s_whi, s_wlo = ([sem(f"weights_{h}{p}") for p in range(PARTS)] for h in ("hi", "lo"))
        s_dve = sem("vector_chain")
        s_xn, s_xt, s_xthi, s_xtlo = sem("xn_made"), sem("xT_made"), sem("xT_hi_made"), sem("xT_lo_made")
        s_up, s_relu, s_hid, s_hhi, s_hlo = sem("up_done"), sem("relu_made"), sem("hid_made"), sem("hid_hi_made"), sem("hid_lo_made")
        s_dn, s_y, s_yn = sem("down_done"), sem("y_made"), sem("y_normed")
        s_pool, s_fin = sem("pool_chain"), sem("ffn_added")
        s_proj, s_projhi, s_projlo = sem("proj_done"), sem("proj_hi_made"), sem("proj_lo_made")
        s_sc, s_max, s_exp, s_rcp = (sem(n) for n in ("scores_done", "max_made", "exp_made", "rcp_made"))
        s_pt, s_pthi, s_ptlo, s_pv = sem("turned"), sem("pT_hi_made"), sem("pT_lo_made"), sem("pv_done")
        s_othi, s_otlo = sem("oT_hi_made"), sem("oT_lo_made")
        s_wo, s_acc, s_out = sem("wo_done"), sem("acc_added"), sem("acc_loaded_or_stored")

        CHAIN = 3 * (8 + 4 * NEWTON) + 2 * NT

        def tile_of(q):
            h = q // 4
            return h, h % 2, (h // 2) % 2, q % 4, 4 * (h % 2) + q % 4

        def slot_of(s):
            h = max(i for i in range(HALVES) if SLOT_BEGIN[i] <= s)
            j, kt = h % 2, s - SLOT_BEGIN[h]
            return h, j, h // 2, kt, max(0, kt - 4 * j)

        def proj_out(u):
            if u < 8:
                h, m, c = u // 4, (u % 4) // 2, u % 2
                return qk_hi[:, h, m, c * CH:(c + 1) * CH], qk_lo[:, h, m, c * CH:(c + 1) * CH], m == 0
            t = 2 * (u - 8)
            flat = "p t h c -> p (t h c)"
            return v_hi[:, t:t + 2].rearrange(flat), v_lo[:, t:t + 2].rearrange(flat), False

        def wo_tiles(i):
            t = 4 * (i // 2 % 2) + 2 * (i % 2)
            return t, t + 1

        def turned(s):
            _, _, _, _, r = slot_of(s)
            if r == TPC - 1:
                return pD_hi[:, P:2 * P], pD_lo[:, P:2 * P], r * P
            return pT_hi[:, s % 3, r * P:CH], pT_lo[:, s % 3, r * P:CH], r * P

        block = ctx.enter_context(nc.Block())

        @block.sync
        def _(sp):
            sp.dma_start(up_raw, up_w.rearrange("(k p) n -> p k n", p=P)).then_inc(s_fraw, 16)
            sp.dma_start(down_raw, down_w.rearrange("(k p) n -> p k n", p=P)).then_inc(s_fraw, 16)
            sp.dma_start(eg_raw[:, :, 0:D], expert_w.rearrange("(k p) n -> p k n", p=P)).then_inc(s_out, 16)
            with nc.allow_non_contiguous_dma(reason="rows of 8 gate weights"):
                sp.dma_start(eg_raw[:, :, D:GW], gate_w.rearrange("(k p) n -> p k n", p=P)).then_inc(s_out, 16)
            sp.dma_start(gamma_b[:, :], gamma.rearrange("(a d) -> a d", a=1).broadcast_to([P, D])).then_inc(s_fraw, 16)
            sp.dma_start(beta_b[:, :], beta.rearrange("(a d) -> a d", a=1).broadcast_to([P, D])).then_inc(s_fraw, 16)
            with sp.Fori(0, B) as b:
                sp.wait_ge(s_fin, b * NT + 1)
                sp.dma_start(xin[:, :, :], x_v[b]).then_inc(s_xin, 16)
                with sp.Fori(0, PAIRS) as g:
                    n = b * PAIRS + g
                    for h, part in ((0, PART_QK0), (1, PART_QK1)):
                        raw = w_raw[:, part, :].rearrange("p (m k c) -> p m k c", m=2, k=KT)
                        sp.wait_ge(s_wlo[part], n + 1)
                        sp.dma_start(raw[:, 0], wq_v[g, h]).then_inc(s_raw[part], 16)
                        sp.dma_start(raw[:, 1], wk_v[g, h]).then_inc(s_raw[part], 16)
                    sp.wait_ge(s_wlo[PART_V], n + 1)
                    sp.dma_start(w_raw[:, PART_V, :].rearrange("p (k c) -> p k c", k=KT), wv_v[g]).then_inc(s_raw[PART_V], 16)
                    sp.wait_ge(s_wlo[PART_O], n + 1)
                    sp.dma_start(w_raw[:, PART_O, :].rearrange("p (s c) -> p s c", s=2), wo_v[g]).then_inc(s_raw[PART_O], 16)

        @block.gpsimd
        def _(pool):
            for part in range(PARTS):
                pool.memset(w_raw[:, part, 0:1], 0.0).then_inc(s_wlo[part], 1)
            pool.memset(xin[:, 0, 0:1], 0.0).then_inc(s_fin, 1)
            pool.memset(ident[:, :], 0.0).then_inc(s_pool, 1)
            pool.memset(mask_bf[:, :], 0.0).then_inc(s_pool, 1)
            pool.wait_ge(s_pool, 2)
            pool.affine_select(out=ident[:, :], in_=ident[:, :], compare_op=ALU.not_equal, fill=1.0, base=0,
                               pattern=[[-1, P]], channel_multiplier=1).then_inc(s_pool, 1)
            pool.affine_select(out=mask_bf[:, :], in_=mask_bf[:, :], compare_op=ALU.is_ge, fill=MASKED, base=0,
                               pattern=[[-1, P]], channel_multiplier=1).then_inc(s_const, 1)
            pool.wait_ge(s_pool, 3)
            pool.tensor_copy(ident_bf[:, :], ident[:, :]).then_inc(s_const, 1)

            def split_lo(n, part):
                pool.wait_ge(s_whi[part], n + 1)
                pool.tensor_tensor(w_lo[:, part, :], w_raw[:, part, :], w_hi[:, part, :], ALU.subtract).then_inc(s_wlo[part], 1)

            pool.wait_ge(s_fraw, 64)
            with pool.Fori(0, B) as b:
                for part in (PART_QK0, PART_QK1, PART_V):
                    split_lo(b * PAIRS, part)
                for t in range(NT):
                    pool.wait_ge(s_yn, b * NT + t + 1)
                    pool.tensor_tensor(y[:, t, :], y[:, t, :], gamma_b[:, :], ALU.mult).then_inc(s_pool, 1)
                    pool.wait_ge(s_pool, b * 2 * NT + 2 * t + 4)
                    pool.tensor_tensor(y[:, t, :], y[:, t, :], beta_b[:, :], ALU.add).then_inc(s_pool, 1)
                    pool.wait_ge(s_pool, b * 2 * NT + 2 * t + 5)
                    if t == 0:
                        pool.wait_ge(s_out, b * 16 + 32)
                    pool.tensor_tensor(acc[:, t, :], y[:, t, :], xin[:, t, :], ALU.add).then_inc(s_fin, 1)
                with pool.Fori(0, PAIRS - 1) as g:
                    n = b * PAIRS + g
                    split_lo(n + 1, PART_QK0)
                    split_lo(n, PART_O)
                    split_lo(n + 1, PART_QK1)
                    split_lo(n + 1, PART_V)
                split_lo(b * PAIRS + PAIRS - 1, PART_O)

        @block.tensor
        def _(pe):
            def three(ps, w_parts, m_parts, first, final):
                for i, (a, c) in enumerate(((0, 1), (1, 0), (0, 0))):
                    mm = pe.matmul(ps, w_parts[a], m_parts[c], start=first and i == 0, stop=final and i == 2)
                return mm

            def xT(k, lo, n):
                return xT_hi[:, k, lo:lo + n], xT_lo[:, k, lo:lo + n]

            def proj_products(ps, u):
                if u < 8:
                    h, m, c = u // 4, (u % 4) // 2, u % 2
                    part = (PART_QK0, PART_QK1)[h]
                    for k in range(KT):
                        at = (m * KT + k) * P
                        mm = three(ps, (w_hi[:, part, at:at + P], w_lo[:, part, at:at + P]), xT(k, c * CH, CH), k == 0, k == KT - 1)
                else:
                    for a in range(2):
                        for k in range(KT):
                            w = slice(k * 2 * P, (k + 1) * 2 * P)
                            mm = three(ps[:, a * 256:(a + 1) * 256], xT(k, (2 * (u - 8) + a) * P, P),
                                       (w_hi[:, PART_V, w], w_lo[:, PART_V, w]), k == 0, k == KT - 1)
                mm.then_inc(s_proj, 1)

            def scores(q):
                _, j, h, _, i = tile_of(q)
                width = (i + 1) * P
                ps = ps_scores[q % 2]
                qs = slice(i * P, (i + 1) * P)
                for c in range(j + 1):
                    w = min(CH, max(width - c * CH, 2 * P))
                    ks = slice(c * CH, c * CH + w)
                    three(ps[:, ks], (qk_hi[:, h, 0, qs], qk_lo[:, h, 0, qs]), (qk_hi[:, h, 1, ks], qk_lo[:, h, 1, ks]), True, c < j)
                pe.matmul(ps[:, qs], ident_bf[:, :], mask_bf[:, :], start=False, stop=True).then_inc(s_sc, 1)

            def step(n, last):
                free = [(s_acc, n * WO_UNITS + 1), (s_projlo, n * UNITS + UNITS), (s_acc, n * WO_UNITS + 1)]
                for kind, i, where in step_order(last):
                    if kind == "scores":
                        if i == 8:
                            pe.wait_ge(s_projlo, n * UNITS + 8)
                        if i == 16:
                            pe.wait_ge(s_projlo, n * UNITS + UNITS + 4)
                        pe.wait_ge(s_exp, n * TILES + i - 1)
                        if tile_of(i)[1] == 1:
                            pe.wait_ge(*free[1 + i % 2])
                            free[1 + i % 2] = (s_exp, n * TILES + i + 1)
                        scores(i)
                    elif kind == "turn":
                        h, j, _, kt, r0 = slot_of(i)
                        if kt == 0:
                            pe.wait_ge(s_exp, n * TILES + 4 * (h + 1))
                        if i >= 2:
                            pe.wait_ge(s_ptlo, n * SLOTS + i - 1)
                        for r in range(r0, TPC):
                            mm = pe.transpose(ps_turn[i % 2][:, r * P:(r + 1) * P], prob[j][:, r, kt * P:(kt + 1) * P], ident[:, :])
                        mm.then_inc(s_pt, 1)
                    elif kind == "pv":
                        h, j, hd, kt, r0 = slot_of(i)
                        if i == 0:
                            pe.wait_ge(s_projlo, n * UNITS + UNITS)
                        if kt == 0:
                            pe.wait_ge(s_otlo, n * HALVES + h + 1)
                        pe.wait_ge(s_ptlo, n * SLOTS + i + 1)
                        if r0 == TPC - 1:
                            m, cols = (pD_hi[:, :], pD_lo[:, :]), slice(CH - 2 * P, CH)
                        else:
                            m, cols = (pT_hi[:, i % 3, r0 * P:CH], pT_lo[:, i % 3, r0 * P:CH]), slice(r0 * P, CH)
                        three(ps_out[:, cols], (v_hi[:, kt, hd, :], v_lo[:, kt, hd, :]), m, kt == 0,
                              kt == 4 * j + 3).then_inc(s_pv, 1)
                    elif kind == "proj":
                        pe.wait_ge(*free[where])
                        if i in (0, 4, 8):
                            pe.wait_ge(s_wlo[(PART_QK0, PART_QK1, PART_V)[i // 4]], n + 3)
                        proj_products(unit_banks[where], i)
                        free[where] = (s_projlo, n * UNITS + UNITS + i + 1)
                    elif kind == "wo":
                        h, w = i // 4, slice(i // 4 * D, (i // 4 + 1) * D)
                        pe.wait_ge(*free[where])
                        if i == 0:
                            pe.wait_ge(s_wlo[PART_O], n + 2)
                        pe.wait_ge(s_otlo, n * HALVES + i // 2 + 2)
                        for a, t in enumerate(wo_tiles(i)):
                            mm = three(unit_banks[where][:, a * D:(a + 1) * D], (oT_hi[:, h, t * P:(t + 1) * P], oT_lo[:, h, t * P:(t + 1) * P]),
                                       (w_hi[:, PART_O, w], w_lo[:, PART_O, w]), True, True)
                        mm.then_inc(s_wo, 1)
                        free[where] = (s_acc, n * WO_UNITS + i + 2)

            pe.wait_ge(s_const, 2)
            with pe.Fori(0, B) as b:
                n0 = b * PAIRS
                pe.wait_ge(s_acc, n0 * WO_UNITS + 1)
                for c in range(NC):
                    pe.wait_ge(s_xn, b * NT + TPC * (c + 1))
                    for k in range(KT):
                        for r in range(TPC):
                            mm = pe.transpose(banks[4 + 2 * c + k][:, r * P:(r + 1) * P],
                                              xn[:, TPC * c + r, k * P:(k + 1) * P], ident[:, :])
                        mm.then_inc(s_xt, 1)
                pe.wait_ge(s_flo, 3)
                for e in range(NC * IT):
                    c, i = e // IT, e % IT
                    if i == 0:
                        pe.wait_ge(s_xtlo, b * 4 + 2 * (c + 1))
                    if e >= 4:
                        pe.wait_ge(s_relu, b * 16 + e - 3)
                    for k in range(KT):
                        w = slice(i * P, (i + 1) * P)
                        mm = three(banks[e % 4], (up_hi[:, k, w], up_lo[:, k, w]), xT(k, c * CH, CH), k == 0, k == KT - 1)
                    mm.then_inc(s_up, 1)
                for t in range(NT):
                    c = t // TPC
                    toks = slice((t % TPC) * P, (t % TPC + 1) * P)
                    if t == 0:
                        pe.wait_ge(s_relu, b * 16 + 16)
                    if t >= 2:
                        pe.wait_ge(s_y, b * NT + t - 1)
                    for k in range(KT):
                        three(banks[2 + t % 2][:, 0:GW], xT(k, t * P, P), (eg_hi[:, k, :], eg_lo[:, k, :]), k == 0, k == KT - 1)
                    if t % TPC == 0:
                        pe.wait_ge(s_hlo, b * 16 + 8 * (c + 1))
                    for i in range(IT):
                        mm = three(banks[t % 2][:, 0:D], (hid_hi[c][:, i, toks], hid_lo[c][:, i, toks]),
                                   (down_hi[:, i, :], down_lo[:, i, :]), i == 0, i == IT - 1)
                    mm.then_inc(s_dn, 1)
                    if t >= TPC:
                        for u in (2 * (t - TPC), 2 * (t - TPC) + 1):
                            if u in (0, 4):
                                pe.wait_ge(s_wlo[u // 4], n0 + 2)
                            if u >= 2:
                                pe.wait_ge(s_projlo, n0 * UNITS + u - 1)
                            proj_products(banks[7 - u % 2], u)
                for kind, i in FIRST_ORDER:
                    if kind == "scores":
                        if i == 0:
                            pe.wait_ge(s_y, b * NT + NT)
                            pe.wait_ge(s_projlo, n0 * UNITS + 4)
                        if i >= 2:
                            pe.wait_ge(s_exp, n0 * TILES + i - 1)
                        scores(i)
                    elif kind == "proj":
                        if i == 8:
                            pe.wait_ge(s_wlo[PART_V], n0 + 2)
                        pe.wait_ge(s_projlo, n0 * UNITS + i - 1)
                        proj_products(banks[7 - i % 2], i)
                with pe.Fori(0, PAIRS - 1) as g:
                    step(b * PAIRS + g, False)
                step(b * PAIRS + PAIRS - 1, True)

        @block.scalar
        def _(act):
            def hi(dst, src, scale=1.0):
                return act.activation(dst, src, ACT.Copy, scale=scale)

            def weights_hi(n, part):
                act.wait_ge(s_raw[part], n * (32 if part <= PART_QK1 else 16) + (32 if part <= PART_QK1 else 16))
                hi(w_hi[:, part, :], w_raw[:, part, :]).then_inc(s_whi[part], 1)

            def proj_hi(ps, n, u):
                dst, _, is_q = proj_out(u)
                act.wait_ge(s_proj, n * UNITS + u + 1)
                hi(dst, ps, SCALE if is_q else 1.0).then_inc(s_projhi, 1)

            def exp(n, q):
                _, j, _, r, i = tile_of(q)
                w = (i + 1) * P
                act.wait_ge(s_max, n * TILES + q + 1)
                act.activation(prob[j][:, r, 0:w], ps_scores[q % 2][:, 0:w], ACT.Exp, bias=neg_max[:, q % TILES:q % TILES + 1],
                               accum_out=prob_sum[:, q % TILES:q % TILES + 1]).then_inc(s_exp, 1)

            def step(n, last):
                for kind, i, where in step_order(last):
                    if kind == "exp":
                        exp(n, i)
                    elif kind == "turn":
                        dst, _, at = turned(i)
                        act.wait_ge(s_pt, n * SLOTS + i + 1)
                        hi(dst, ps_turn[i % 2][:, at:CH]).then_inc(s_pthi, 1)
                    elif kind == "out":
                        act.wait_ge(s_pv, n * SLOTS + SLOT_BEGIN[i + 1])
                        hi(oT_hi[:, i // 2, (i % 2) * CH:(i % 2 + 1) * CH], ps_out[:, :]).then_inc(s_othi, 1)
                    elif kind == "weights":
                        if i == PART_O:
                            act.wait_ge(s_acc, n * WO_UNITS + 1)
                        weights_hi(n if i == PART_O else n + 1, i)
                    elif kind == "proj":
                        proj_hi(unit_banks[where], n + 1, i)

            act.wait_ge(s_fraw, 64)
            act.wait_ge(s_out, 32)
            hi(up_hi[:, :, :], up_raw).then_inc(s_fhi, 1)
            hi(down_hi[:, :, :], down_raw).then_inc(s_fhi, 1)
            hi(eg_hi[:, :, :], eg_raw).then_inc(s_fhi, 1)
            with act.Fori(0, B) as b:
                n0 = b * PAIRS
                for part in (PART_QK0, PART_QK1, PART_V):
                    weights_hi(n0, part)
                for g in range(4):
                    act.wait_ge(s_xt, b * 4 + g + 1)
                    hi(xT_hi[:, g % 2, (g // 2) * CH:(g // 2 + 1) * CH], banks[4 + g]).then_inc(s_xthi, 1)

                def hidden_hi(e):
                    act.wait_ge(s_hid, b * 16 + e + 1)
                    hi(hid_hi[e // IT][:, e % IT, :], hid[:, e % IT, :]).then_inc(s_hhi, 1)

                for e in range(NC * IT):
                    if e >= IT:
                        act.wait_ge(s_hlo, b * 16 + e - IT + 1)
                    act.wait_ge(s_up, b * 16 + e + 1)
                    act.activation(hid[:, e % IT, :], banks[e % 4], ACT.Relu).then_inc(s_relu, 1)
                    if e > 0:
                        hidden_hi(e - 1)
                hidden_hi(NC * IT - 1)
                for u in range(8):
                    proj_hi(banks[7 - u % 2], n0, u)
                for kind, i in FIRST_ORDER:
                    if kind == "exp":
                        exp(n0, i)
                    elif kind == "proj":
                        proj_hi(banks[7 - i % 2], n0, i)
                with act.Fori(0, PAIRS - 1) as g:
                    step(b * PAIRS + g, False)
                step(b * PAIRS + PAIRS - 1, True)
                act.wait_ge(s_acc, b * PAIRS * WO_UNITS + PAIRS * WO_UNITS + 1)
                act.dma_start(out_v[b], acc[:, :, :]).then_inc(s_out, 16)
            act.wait_ge(s_out, 16 * B + 32)

        @block.vector
        def _(dve):
            def proj_lo(ps, n, u):
                h_, l_, is_q = proj_out(u)
                dve.wait_ge(s_projhi, n * UNITS + u + 1)
                if is_q:
                    ins = dve.scalar_tensor_tensor(out=l_, in0=ps, scalar=SCALE, in1=h_, op0=ALU.mult, op1=ALU.subtract)
                else:
                    ins = dve.tensor_tensor(l_, ps, h_, ALU.subtract)
                ins.then_inc(s_projlo, 1)

            def maximum(n, q):
                _, _, _, _, i = tile_of(q)
                dve.wait_ge(s_sc, n * TILES + q + 1)
                dve.tensor_reduce(neg_max[:, q % TILES:q % TILES + 1], ps_scores[q % 2][:, 0:(i + 1) * P], AX.X, ALU.max,
                                  negate=True).then_inc(s_max, 1)

            def step(n, last):
                for kind, i, where in step_order(last):
                    if kind == "scores":
                        maximum(n, i)
                    elif kind == "turn":
                        h_, l_, at = turned(i)
                        dve.wait_ge(s_pthi, n * SLOTS + i + 1)
                        dve.tensor_tensor(l_, ps_turn[i % 2][:, at:CH], h_, ALU.subtract).then_inc(s_ptlo, 1)
                    elif kind == "out":
                        cols = slice((i % 2) * CH, (i % 2 + 1) * CH)
                        dve.wait_ge(s_othi, n * HALVES + i + 1)
                        dve.tensor_tensor(oT_lo[:, i // 2, cols], ps_out[:, :], oT_hi[:, i // 2, cols], ALU.subtract).then_inc(s_otlo, 1)
                        four = slice(4 * i, 4 * i + 4)
                        dve.reciprocal(prob_rcp[:, four], prob_sum[:, four]).then_inc(s_rcp, 1)
                    elif kind == "proj":
                        proj_lo(unit_banks[where], n + 1, i)
                    elif kind == "wo":
                        dve.wait_ge(s_rcp, n * HALVES + i // 2 + 1)
                        dve.wait_ge(s_acc, n * WO_UNITS + (1 if i < 4 else i - 2))
                        dve.wait_ge(s_wo, n * WO_UNITS + i + 1)
                        for a, t in enumerate(wo_tiles(i)):
                            q = 4 * (i // 2) + t % 4
                            last_add = dve.scalar_tensor_tensor(out=acc[:, t, :], in0=unit_banks[where][:, a * D:(a + 1) * D],
                                                                scalar=prob_rcp[:, q:q + 1], in1=acc[:, t, :], op0=ALU.mult, op1=ALU.add)
                        last_add.then_inc(s_acc, 1)

            dve.memset(ps_out[:, 0:1], 0.0).then_inc(s_otlo, 1)
            dve.memset(ps_proj[:, 0:1], 0.0).then_inc(s_acc, 1)
            dve.memset(pD_hi[:, 0:P].bitcast(F32), 0.0).then_inc(s_dve, 1)
            dve.memset(pD_lo[:, 0:P].bitcast(F32), 0.0).then_inc(s_dve, 1)
            for i, (raw, h_, l_) in enumerate(((up_raw, up_hi, up_lo), (down_raw, down_hi, down_lo), (eg_raw, eg_hi, eg_lo))):
                dve.wait_ge(s_fhi, i + 1)
                dve.tensor_tensor(l_[:, :, :], raw, h_[:, :, :], ALU.subtract).then_inc(s_flo, 1)
            dve.wait_ge(s_flo, 3)
            with dve.Fori(0, B) as b:
                n0 = b * PAIRS
                done = [2]

                def link(ins):
                    done[0] += 1
                    ins.then_inc(s_dve, 1)
                    dve.wait_ge(s_dve, b * CHAIN + done[0])

                def moments(src, lo, k):
                    ts = slice(lo, lo + k)
                    st = stats[:, ts, :]
                    for t in range(lo, lo + k):
                        last = dve.bn_stats(stats[:, t, :], src[:, t, :])
                    link(last)
                    link(dve.tensor_tensor(tmp[:, ts], st[:, :, 1], st[:, :, 4], ALU.subtract))
                    dve.tensor_tensor(mean[:, ts], st[:, :, 1], st[:, :, 4], ALU.add)
                    dve.tensor_tensor(half[:, ts], st[:, :, 2], st[:, :, 5], ALU.add)
                    link(dve.scalar_tensor_tensor(out=var[:, ts], in0=tmp[:, ts], scalar=0.25, in1=tmp[:, ts], op0=ALU.mult, op1=ALU.mult))
                    link(dve.scalar_tensor_tensor(out=half[:, ts], in0=half[:, ts], scalar=1.0 / D, in1=var[:, ts], op0=ALU.mult, op1=ALU.add))
                    dve.tensor_scalar(mean[:, ts], mean[:, ts], 0.5, None, ALU.mult)
                    link(dve.tensor_scalar(var[:, ts], half[:, ts], EPS, None, ALU.add))
                    link(dve.tensor_scalar(half[:, ts].bitcast(I32), var[:, ts].bitcast(I32), 1, None, ALU.logical_shift_right))
                    link(dve.tensor_scalar(rstd[:, ts].bitcast(I32), half[:, ts].bitcast(I32), -1.0, RSQRT_GUESS, ALU.mult, ALU.add))
                    link(dve.tensor_scalar(half[:, ts], var[:, ts], 0.5, None, ALU.mult))
                    for _ in range(NEWTON):
                        link(dve.tensor_tensor(tmp[:, ts], rstd[:, ts], rstd[:, ts], ALU.mult))
                        link(dve.tensor_tensor(tmp[:, ts], tmp[:, ts], half[:, ts], ALU.mult))
                        link(dve.tensor_scalar(tmp[:, ts], tmp[:, ts], -1.0, 1.5, ALU.mult, ALU.add))
                        link(dve.tensor_tensor(rstd[:, ts], tmp[:, ts], rstd[:, ts], ALU.mult))

                def feed_forward_sum(t):
                    dve.wait_ge(s_dn, b * NT + t + 1)
                    dve.tensor_copy(y[:, t, :], banks[t % 2][:, 0:D])
                    link(dve.max(top8[:, t, :], banks[2 + t % 2][:, D:GW]))
                    link(dve.tensor_tensor(top2[:, t:t + 1], top8[:, t, 0:1], top8[:, t, 1:2], ALU.add))
                    dve.scalar_tensor_tensor(out=y[:, t, :], in0=banks[2 + t % 2][:, 0:D], scalar=top2[:, t:t + 1], in1=y[:, t, :],
                                             op0=ALU.mult, op1=ALU.add).then_inc(s_y, 1)

                def normed_y(c):
                    dve.wait_ge(s_y, b * NT + TPC * (c + 1))
                    moments(y, TPC * c, TPC)
                    for t in range(TPC * c, TPC * (c + 1)):
                        dve.tensor_scalar(y[:, t, :], y[:, t, :], mean[:, t:t + 1], rstd[:, t:t + 1],
                                          ALU.subtract, ALU.mult).then_inc(s_yn, 1)

                dve.wait_ge(s_xin, b * 16 + 16)
                moments(xin, 0, NT)
                for t in range(NT):
                    dve.tensor_scalar(xn[:, t, :], xin[:, t, :], mean[:, t:t + 1], rstd[:, t:t + 1],
                                      ALU.subtract, ALU.mult).then_inc(s_xn, 1)
                for g in range(4):
                    dst = slice((g // 2) * CH, (g // 2 + 1) * CH)
                    dve.wait_ge(s_xthi, b * 4 + g + 1)
                    dve.tensor_tensor(xT_lo[:, g % 2, dst], banks[4 + g], xT_hi[:, g % 2, dst], ALU.subtract).then_inc(s_xtlo, 1)

                def hidden_lo(e):
                    dve.wait_ge(s_hhi, b * 16 + e + 1)
                    dve.tensor_tensor(hid_lo[e // IT][:, e % IT, :], hid[:, e % IT, :], hid_hi[e // IT][:, e % IT, :],
                                      ALU.subtract).then_inc(s_hlo, 1)

                for e in range(NC * IT):
                    dve.wait_ge(s_relu, b * 16 + e + 1)
                    r = hid[:, e % IT, :]
                    dve.tensor_tensor(r, r, r, ALU.mult).then_inc(s_hid, 1)
                    if e > 0:
                        hidden_lo(e - 1)
                hidden_lo(NC * IT - 1)
                for t in range(NT):
                    feed_forward_sum(t)
                    if t == TPC - 1:
                        normed_y(0)
                    if t >= TPC:
                        proj_lo(banks[7 - 0], n0, 2 * (t - TPC))
                        proj_lo(banks[7 - 1], n0, 2 * (t - TPC) + 1)
                normed_y(1)
                assert done[0] - 2 == CHAIN, done[0] - 2
                for kind, i in FIRST_ORDER:
                    if kind == "scores":
                        maximum(n0, i)
                    elif kind == "proj":
                        proj_lo(banks[7 - i % 2], n0, i)
                with dve.Fori(0, PAIRS - 1) as g:
                    step(b * PAIRS + g, False)
                step(b * PAIRS + PAIRS - 1, True)


_INS = ["L0_attn_hidden_states", "L0_attn_Wq", "L0_attn_Wk", "L0_attn_Wv", "L0_attn_Wo", "L0_ffn_gate_w",
        "L0_ffn_up_w", "L0_ffn_down_w", "L0_ffn_expert_weight", "L0_ffn_ln_gamma", "L0_ffn_ln_beta"]


def kernel(**inputs):
    import numpy as _np
    import concourse.bacc as _bacc
    from concourse import mybir as _mybir
    from concourse.bass_utils import run_bass_kernel_spmd as _run

    nc = _bacc.Bacc("TRN2", target_bir_lowering=False, num_devices=1)
    arrays, args = {}, []
    for name in _INS:
        a = _np.ascontiguousarray(inputs[name])
        arrays[f"in_{name}_dram"] = a
        args.append(nc.dram_tensor(f"in_{name}_dram", a.shape, _mybir.dt.from_np(a.dtype), kind="ExternalInput").ap())
    shape = inputs[_INS[0]].shape
    out = nc.dram_tensor("out_0_dram", shape, _mybir.dt.float32, kind="ExternalOutput").ap()
    layer_kernel(nc, *args, out)
    r = _run(nc, [arrays], core_ids=[0])
    return r.results[0]["out_0_dram"]
```

```python
from contextlib import ExitStack

import concourse.bass as bass
from concourse import mybir

F32 = mybir.dt.float32
F32R = mybir.dt.float32r
BF16 = mybir.dt.bfloat16
I32 = mybir.dt.int32
ALU = mybir.AluOpType
ACT = mybir.ActivationFunctionType
AX = mybir.AxisListType

P = 128
EPS = 1e-5
MASKED = -1e30
RSQRT_GUESS = float(0x5F3759DF)
NEWTON = 3

TILES = 16
SLOTS = 24
UNITS = 12
HALVES = 4
WO_UNITS = 8
PARTS = 4
SLOT_BEGIN = [0, 4, 12, 16, 24]
PART_QK0, PART_QK1, PART_V, PART_O = range(4)


PROJ_BANK, SPARE0, SPARE1, TURN0, TURN1 = range(5)
SPARES = (SPARE0, SPARE1)


def step_order(last):
    scores = {0: [4, 5], 1: [6], 2: [7], 4: [8], 5: [9], 6: [10], 8: [11],
              12: [12, 13], 13: [14], 14: [15], 16: [16], 17: [17], 18: [18], 19: [19]}
    weights = {0: PART_QK0, 3: PART_O, 6: PART_QK1, 9: PART_V}
    units = {3: [("proj", 0, PROJ_BANK), ("proj", 1, SPARE0)], 4: [("proj", 2, SPARE1)],
             7: [("wo", 0, PROJ_BANK)], 9: [("wo", 1, SPARE0)], 10: [("proj", 3, SPARE1)],
             13: [("wo", 2, PROJ_BANK)], 14: [("proj", 4, PROJ_BANK)],
             15: [("proj", 5, SPARE0), ("wo", 3, PROJ_BANK)], 16: [("proj", 6, SPARE1)],
             18: [("wo", 4, PROJ_BANK)], 20: [("wo", 5, SPARE0)],
             21: [("proj", 7, SPARE1)], 22: [("proj", 8, PROJ_BANK)], 23: [("proj", 9, SPARE1)]}
    if last:
        norms = {s: [("moments", i, None)] for i, s in enumerate((4, 5, 7, 8, 9, 10, 11, 12, 13))}
        norms |= {16: [("normed", 0, None)], 17: [("normed", 1, None)], 18: [("xturn", 0, SPARE1)], 19: [("xturn", 1, SPARE0)]}
        moved = {13: [], 14: [], 15: [("wo", 2, PROJ_BANK), ("wo", 3, SPARE0)]}
        units = {s: moved.get(s, units.get(s, [])) + norms.get(s, []) for s in range(SLOTS)}
    order = [("turn", 0, None)]
    for s in range(SLOTS):
        first, end = s in SLOT_BEGIN, s + 1 in SLOT_BEGIN
        now = [q for q in scores.get(s, []) if not (last and q >= TILES)]
        order += [("scores", q, None) for q in now]
        order += [u for u in units.get(s, []) if not (last and u[0] == "proj")]
        if first:
            order += [("exp", q, None) for q in now[:1]]
            order.append(("turn", s + 1, None))
            now = now[1:]
        if s + 2 not in SLOT_BEGIN and s + 1 < SLOTS:
            order.append(("turn", s + 1 if end else s + 2, None))
        order += [("exp", q, None) for q in now]
        if s in weights and not (last and weights[s] != PART_O):
            order.append(("weights", weights[s], None))
        order.append(("pv", s, None))
        if end:
            order.append(("out", SLOT_BEGIN.index(s + 1) - 1, None))
    if not last:
        return order + [("proj", 10, SPARE0), ("proj", 11, PROJ_BANK), ("wo", 6, SPARE1), ("wo", 7, TURN1)]
    return order + [("xturn", 2, SPARE1), ("xturn", 3, PROJ_BANK), ("wo", 6, SPARE0), ("wo", 7, TURN0)]


FIRST_ORDER = [("proj", 0), ("proj", 1), ("moments", 0), ("proj", 2), ("moments", 1), ("proj", 3), ("moments", 4),
               ("scores", 0), ("exp", 0), ("proj", 4), ("moments", 5), ("scores", 1), ("exp", 1), ("proj", 5), ("moments", 6),
               ("scores", 2), ("exp", 2), ("proj", 6), ("moments", 7), ("scores", 3), ("exp", 3), ("proj", 7), ("moments", 8),
               ("proj", 8), ("normed", 1), ("proj", 9), ("proj", 10), ("proj", 11)]


def layer_kernel(nc, x, wq, wk, wv, wo, gate_w, up_w, down_w, expert_w, gamma, beta, out):
    B, S, D = x.shape
    HEADS_D = wq.shape[1]
    INTER = up_w.shape[1]
    EXPERTS = gate_w.shape[1]
    KT = D // P
    NT = S // P
    CH = 512
    NC = S // CH
    TPC = CH // P
    IT = INTER // P
    PAIRS = HEADS_D // (2 * P)
    SCALE = float(P) ** -0.5
    GW = D + EXPERTS
    assert (D, S, KT, NT, NC, IT) == (256, 1024, 2, 8, 2, 8)

    x_v = x.rearrange("b (t p) d -> b p t d", p=P)
    out_v = out.rearrange("b (t p) d -> b p t d", p=P)
    wq_v = wq.rearrange("(k p) (g s c) -> g s p k c", p=P, s=2, c=P)
    wk_v = wk.rearrange("(k p) (g s c) -> g s p k c", p=P, s=2, c=P)
    wv_v = wv.rearrange("(k p) (g c) -> g p k c", p=P, c=2 * P)
    wo_v = wo.rearrange("(g s p) n -> g p s n", p=P, s=2)

    with ExitStack() as ctx:
        def sb(name, shape, dt=F32):
            return ctx.enter_context(nc.sbuf_tensor(name, shape, dt))

        def bank(name, n=1):
            return ctx.enter_context(nc.psum_tensor(name, [P, 512 * n], F32))

        def sem(name):
            return ctx.enter_context(nc.semaphore(name))

        xT_hi, xT_lo = (sb(f"xT_{h}", [P, KT, S], F32R) for h in ("hi", "lo"))
        shared = sb("shared", [P, 16384], F32R)
        qk_hi = shared[:, 0:4096].rearrange("p (h m s) -> p h m s", h=2, m=2)
        qk_lo = shared[:, 4096:8192].rearrange("p (h m s) -> p h m s", h=2, m=2)
        v_hi = shared[:, 8192:10240].rearrange("p (t h c) -> p t h c", t=NT, h=2)
        v_lo = shared[:, 10240:12288].rearrange("p (t h c) -> p t h c", t=NT, h=2)
        oT_hi = shared[:, 12288:14336].rearrange("p (h s) -> p h s", h=2)
        oT_lo = shared[:, 14336:16384].rearrange("p (h s) -> p h s", h=2)
        hid_hi = [shared[:, 8192 * c:8192 * c + 4096].rearrange("p (i s) -> p i s", i=IT) for c in range(NC)]
        hid_lo = [shared[:, 8192 * c + 4096:8192 * c + 8192].rearrange("p (i s) -> p i s", i=IT) for c in range(NC)]
        prob = [sb("prob0", [P, TPC, CH]), sb("prob1", [P, TPC, S])]
        xn = prob[0][:, :, :].rearrange("p r (a d) -> p (r a) d", a=2)
        hid = prob[1][:, :, :].rearrange("p r (a s) -> p (r a) s", a=2)
        pT_hi, pT_lo = (sb(f"pT_{h}", [P, 3, CH], F32R) for h in ("hi", "lo"))
        pD_hi, pD_lo = (sb(f"pD_{h}", [P, 2 * P], F32R) for h in ("hi", "lo"))
        w_raw = sb("w_raw", [P, PARTS, 512])
        w_hi, w_lo = (sb(f"w_{h}", [P, PARTS, 512], F32R) for h in ("hi", "lo"))
        up_hi, up_lo = (sb(f"up_{h}", [P, KT, INTER], F32R) for h in ("hi", "lo"))
        down_hi, down_lo = (sb(f"down_{h}", [P, IT, D], F32R) for h in ("hi", "lo"))
        eg_hi, eg_lo = (sb(f"eg_{h}", [P, KT, GW], F32R) for h in ("hi", "lo"))
        up_raw = prob[1][:, 0:2, :]
        down_raw = prob[1][:, 2:4, :].rearrange("p r (a n) -> p (r a) n", n=D)
        acc = sb("acc", [P, NT, D])
        eg_raw = acc[:, :, :].rearrange("p t d -> p (t d)")[:, 0:KT * GW].rearrange("p (k n) -> p k n", k=KT)
        xin = sb("xin", [P, NT, D])
        y = sb("y", [P, NT, D])
        gamma_b, beta_b = sb("gamma_b", [P, D]), sb("beta_b", [P, D])
        ident = sb("ident", [P, P])
        ident_bf, mask_bf = sb("ident_bf", [P, P], BF16), sb("mask_bf", [P, P], BF16)
        stats = sb("stats", [P, NT, 6])
        mean, var, rstd, tmp, half = (sb(n, [P, NT]) for n in ("mean", "var", "rstd", "tmp", "half"))
        mean_x, rstd_x = sb("mean_x", [P, NT]), sb("rstd_x", [P, NT])
        top8 = sb("top8", [P, NT, 8])
        top2 = sb("top2", [P, NT])
        neg_max, prob_sum, prob_rcp = (sb(n, [P, TILES]) for n in ("neg_max", "prob_sum", "prob_rcp"))

        ps_scores = [bank("ps_scores0", 2), bank("ps_scores1", 2)]
        ps_turn = [bank("ps_turn0"), bank("ps_turn1")]
        ps_out, ps_proj = bank("ps_out"), bank("ps_proj")
        banks = [ps_scores[0][:, 0:512], ps_scores[0][:, 512:1024], ps_scores[1][:, 0:512],
                 ps_scores[1][:, 512:1024], ps_turn[0][:, :], ps_turn[1][:, :], ps_out[:, :], ps_proj[:, :]]

        unit_banks = [banks[7], banks[1], banks[3], banks[4], banks[5]]

        s_const = sem("constants_made")
        s_fraw = sem("ffn_weights_loaded")
        s_fhi, s_flo = sem("ffn_weights_hi"), sem("ffn_weights_lo")
        s_xin = sem("x_loaded")
        s_raw = [sem(f"weights_loaded{p}") for p in range(PARTS)]
        s_whi, s_wlo = ([sem(f"weights_{h}{p}") for p in range(PARTS)] for h in ("hi", "lo"))
        s_dve = sem("vector_chain")
        s_xn, s_xt, s_xthi, s_xtlo = sem("xn_made"), sem("xT_made"), sem("xT_hi_made"), sem("xT_lo_made")
        s_up, s_relu, s_hid, s_hhi, s_hlo = sem("up_done"), sem("relu_made"), sem("hid_made"), sem("hid_hi_made"), sem("hid_lo_made")
        s_dn, s_y, s_yn = sem("down_done"), sem("y_made"), sem("y_normed")
        s_pool, s_fin = sem("pool_chain"), sem("ffn_added")
        s_proj, s_projhi, s_projlo = sem("proj_done"), sem("proj_hi_made"), sem("proj_lo_made")
        s_sc, s_max, s_exp, s_rcp = (sem(n) for n in ("scores_done", "max_made", "exp_made", "rcp_made"))
        s_pt, s_pthi, s_ptlo, s_pv = sem("turned"), sem("pT_hi_made"), sem("pT_lo_made"), sem("pv_done")
        s_othi, s_otlo = sem("oT_hi_made"), sem("oT_lo_made")
        s_wo, s_acc, s_out = sem("wo_done"), sem("acc_added"), sem("acc_loaded_or_stored")

        MOMENTS = 8 + 3 * NEWTON
        STATS = NT // 2
        MOMENT_PARTS = STATS + 2 + NEWTON
        CHAIN = 3 * MOMENTS + 2 * NT

        def tile_of(q):
            h = q // 4
            return h, h % 2, (h // 2) % 2, q % 4, 4 * (h % 2) + q % 4

        def slot_of(s):
            h = max(i for i in range(HALVES) if SLOT_BEGIN[i] <= s)
            j, kt = h % 2, s - SLOT_BEGIN[h]
            return h, j, h // 2, kt, max(0, kt - 4 * j)

        def proj_out(u):
            if u < 8:
                h, m, c = u // 4, (u % 4) // 2, u % 2
                return qk_hi[:, h, m, c * CH:(c + 1) * CH], qk_lo[:, h, m, c * CH:(c + 1) * CH], m == 0
            t = 2 * (u - 8)
            flat = "p t h c -> p (t h c)"
            return v_hi[:, t:t + 2].rearrange(flat), v_lo[:, t:t + 2].rearrange(flat), False

        def wo_tiles(i):
            t = 4 * (i // 2 % 2) + 2 * (i % 2)
            return t, t + 1

        def turned(s):
            _, _, _, _, r = slot_of(s)
            if r == TPC - 1:
                return pD_hi[:, P:2 * P], pD_lo[:, P:2 * P], r * P
            return pT_hi[:, s % 3, r * P:CH], pT_lo[:, s % 3, r * P:CH], r * P

        block = ctx.enter_context(nc.Block())

        @block.sync
        def _(sp):
            sp.dma_start(xin[:, :, :], x_v[0]).then_inc(s_xin, 16)
            sp.dma_start(up_raw, up_w.rearrange("(k p) n -> p k n", p=P)).then_inc(s_fraw, 16)
            sp.dma_start(down_raw, down_w.rearrange("(k p) n -> p k n", p=P)).then_inc(s_fraw, 16)
            sp.dma_start(eg_raw[:, :, 0:D], expert_w.rearrange("(k p) n -> p k n", p=P)).then_inc(s_out, 16)
            with nc.allow_non_contiguous_dma(reason="rows of 8 gate weights"):
                sp.dma_start(eg_raw[:, :, D:GW], gate_w.rearrange("(k p) n -> p k n", p=P)).then_inc(s_out, 16)
            sp.dma_start(gamma_b[:, :], gamma.rearrange("(a d) -> a d", a=1).broadcast_to([P, D])).then_inc(s_fraw, 16)
            sp.dma_start(beta_b[:, :], beta.rearrange("(a d) -> a d", a=1).broadcast_to([P, D])).then_inc(s_fraw, 16)
            with sp.Fori(0, B) as b:
                with sp.Fori(0, PAIRS) as g:
                    n = b * PAIRS + g
                    for h, part in ((0, PART_QK0), (1, PART_QK1)):
                        raw = w_raw[:, part, :].rearrange("p (m k c) -> p m k c", m=2, k=KT)
                        sp.wait_ge(s_wlo[part], n + 1)
                        sp.dma_start(raw[:, 0], wq_v[g, h]).then_inc(s_raw[part], 16)
                        sp.dma_start(raw[:, 1], wk_v[g, h]).then_inc(s_raw[part], 16)
                    sp.wait_ge(s_wlo[PART_V], n + 1)
                    sp.dma_start(w_raw[:, PART_V, :].rearrange("p (k c) -> p k c", k=KT), wv_v[g]).then_inc(s_raw[PART_V], 16)
                    sp.wait_ge(s_wlo[PART_O], n + 1)
                    sp.dma_start(w_raw[:, PART_O, :].rearrange("p (s c) -> p s c", s=2), wo_v[g]).then_inc(s_raw[PART_O], 16)
                sp.wait_ge(s_fin, b * NT + NT)
                sp.dma_start(xin[:, :, :], x_v[(b + 1) % B]).then_inc(s_xin, 16)

        @block.gpsimd
        def _(pool):
            for part in range(PARTS):
                pool.memset(w_raw[:, part, 0:1], 0.0).then_inc(s_wlo[part], 1)
            pool.memset(ident[:, :], 0.0).then_inc(s_pool, 1)
            pool.memset(mask_bf[:, :], 0.0).then_inc(s_pool, 1)
            pool.wait_ge(s_pool, 2)
            pool.affine_select(out=ident[:, :], in_=ident[:, :], compare_op=ALU.not_equal, fill=1.0, base=0,
                               pattern=[[-1, P]], channel_multiplier=1).then_inc(s_pool, 1)
            pool.affine_select(out=mask_bf[:, :], in_=mask_bf[:, :], compare_op=ALU.is_ge, fill=MASKED, base=0,
                               pattern=[[-1, P]], channel_multiplier=1).then_inc(s_const, 1)
            pool.wait_ge(s_pool, 3)
            pool.tensor_copy(ident_bf[:, :], ident[:, :]).then_inc(s_const, 1)

            def split_lo(n, part):
                pool.wait_ge(s_whi[part], n + 1)
                pool.tensor_tensor(w_lo[:, part, :], w_raw[:, part, :], w_hi[:, part, :], ALU.subtract).then_inc(s_wlo[part], 1)

            for i, (raw, h_, l_) in enumerate(((up_raw, up_hi, up_lo), (down_raw, down_hi, down_lo), (eg_raw, eg_hi, eg_lo))):
                pool.wait_ge(s_fhi, i + 1)
                pool.tensor_tensor(l_[:, :, :], raw, h_[:, :, :], ALU.subtract).then_inc(s_flo, 1)
            pool.wait_ge(s_fraw, 64)
            with pool.Fori(0, B) as b:
                for part in (PART_QK0, PART_QK1, PART_V):
                    split_lo(b * PAIRS, part)
                for t in range(NT):
                    pool.wait_ge(s_yn, b * NT + t + 1)
                    pool.tensor_tensor(y[:, t, :], y[:, t, :], gamma_b[:, :], ALU.mult).then_inc(s_pool, 1)
                    pool.wait_ge(s_pool, b * 2 * NT + 2 * t + 4)
                    pool.tensor_tensor(y[:, t, :], y[:, t, :], beta_b[:, :], ALU.add).then_inc(s_pool, 1)
                    pool.wait_ge(s_pool, b * 2 * NT + 2 * t + 5)
                    if t == 0:
                        pool.wait_ge(s_out, b * 16 + 32)
                        pool.wait_ge(s_flo, 3)
                    pool.tensor_tensor(acc[:, t, :], y[:, t, :], xin[:, t, :], ALU.add).then_inc(s_fin, 1)
                with pool.Fori(0, PAIRS - 1) as g:
                    n = b * PAIRS + g
                    split_lo(n + 1, PART_QK0)
                    split_lo(n, PART_O)
                    split_lo(n + 1, PART_QK1)
                    split_lo(n + 1, PART_V)
                split_lo(b * PAIRS + PAIRS - 1, PART_O)

        @block.tensor
        def _(pe):
            def three(ps, w_parts, m_parts, first, final):
                for i, (a, c) in enumerate(((0, 1), (1, 0), (0, 0))):
                    mm = pe.matmul(ps, w_parts[a], m_parts[c], start=first and i == 0, stop=final and i == 2)
                return mm

            def xT(k, lo, n):
                return xT_hi[:, k, lo:lo + n], xT_lo[:, k, lo:lo + n]

            def proj_products(ps, u):
                if u < 8:
                    h, m, c = u // 4, (u % 4) // 2, u % 2
                    part = (PART_QK0, PART_QK1)[h]
                    for k in range(KT):
                        at = (m * KT + k) * P
                        mm = three(ps, (w_hi[:, part, at:at + P], w_lo[:, part, at:at + P]), xT(k, c * CH, CH), k == 0, k == KT - 1)
                else:
                    for a in range(2):
                        for k in range(KT):
                            w = slice(k * 2 * P, (k + 1) * 2 * P)
                            mm = three(ps[:, a * 256:(a + 1) * 256], xT(k, (2 * (u - 8) + a) * P, P),
                                       (w_hi[:, PART_V, w], w_lo[:, PART_V, w]), k == 0, k == KT - 1)
                mm.then_inc(s_proj, 1)

            def scores(q):
                _, j, h, _, i = tile_of(q)
                width = (i + 1) * P
                ps = ps_scores[q % 2]
                qs = slice(i * P, (i + 1) * P)
                for c in range(j + 1):
                    w = min(CH, max(width - c * CH, 2 * P))
                    ks = slice(c * CH, c * CH + w)
                    three(ps[:, ks], (qk_hi[:, h, 0, qs], qk_lo[:, h, 0, qs]), (qk_hi[:, h, 1, ks], qk_lo[:, h, 1, ks]), True, c < j)
                pe.matmul(ps[:, qs], ident_bf[:, :], mask_bf[:, :], start=False, stop=True).then_inc(s_sc, 1)

            def step(b, n, last):
                free = {PROJ_BANK: (s_projlo, n * UNITS + UNITS), SPARE0: (s_projlo, n * UNITS + UNITS - 1), SPARE1: (s_acc, n * WO_UNITS + 1),
                        TURN0: (s_ptlo, n * SLOTS + SLOTS - 1), TURN1: (s_ptlo, n * SLOTS + SLOTS)}
                for kind, i, where in step_order(last):
                    if kind == "scores":
                        if i == 8:
                            pe.wait_ge(s_projlo, n * UNITS + 8)
                        if i == 16:
                            pe.wait_ge(s_projlo, n * UNITS + UNITS + 4)
                        pe.wait_ge(s_exp, n * TILES + i - 1)
                        if tile_of(i)[1] == 1:
                            pe.wait_ge(*free[SPARES[i % 2]])
                            free[SPARES[i % 2]] = (s_exp, n * TILES + i + 1)
                        scores(i)
                    elif kind == "turn":
                        h, j, _, kt, r0 = slot_of(i)
                        if i == 0:
                            pe.wait_ge(s_projlo, n * UNITS + 10)
                        if i == 1:
                            pe.wait_ge(s_acc, n * WO_UNITS + 1)
                        if kt == 0:
                            pe.wait_ge(s_exp, n * TILES + 4 * (h + 1))
                        if i >= 2:
                            pe.wait_ge(s_ptlo, n * SLOTS + i - 1)
                        for r in range(r0, TPC):
                            mm = pe.transpose(ps_turn[i % 2][:, r * P:(r + 1) * P], prob[j][:, r, kt * P:(kt + 1) * P], ident[:, :])
                        mm.then_inc(s_pt, 1)
                    elif kind == "pv":
                        h, j, hd, kt, r0 = slot_of(i)
                        if i == 0:
                            pe.wait_ge(s_projlo, n * UNITS + UNITS)
                        if kt == 0:
                            pe.wait_ge(s_otlo, n * HALVES + h + 1)
                        pe.wait_ge(s_ptlo, n * SLOTS + i + 1)
                        if r0 == TPC - 1:
                            m, cols = (pD_hi[:, :], pD_lo[:, :]), slice(CH - 2 * P, CH)
                        else:
                            m, cols = (pT_hi[:, i % 3, r0 * P:CH], pT_lo[:, i % 3, r0 * P:CH]), slice(r0 * P, CH)
                        three(ps_out[:, cols], (v_hi[:, kt, hd, :], v_lo[:, kt, hd, :]), m, kt == 0,
                              kt == 4 * j + 3).then_inc(s_pv, 1)
                    elif kind == "proj":
                        pe.wait_ge(*free[where])
                        if i in (0, 4, 8):
                            pe.wait_ge(s_wlo[(PART_QK0, PART_QK1, PART_V)[i // 4]], n + 3)
                        proj_products(unit_banks[where], i)
                        free[where] = (s_projlo, n * UNITS + UNITS + i + 1)
                    elif kind == "wo":
                        h, w = i // 4, slice(i // 4 * D, (i // 4 + 1) * D)
                        pe.wait_ge(*free[where])
                        if i == 0:
                            pe.wait_ge(s_wlo[PART_O], n + 2)
                        pe.wait_ge(s_otlo, n * HALVES + i // 2 + 2)
                        for a, t in enumerate(wo_tiles(i)):
                            mm = three(unit_banks[where][:, a * D:(a + 1) * D], (oT_hi[:, h, t * P:(t + 1) * P], oT_lo[:, h, t * P:(t + 1) * P]),
                                       (w_hi[:, PART_O, w], w_lo[:, PART_O, w]), True, True)
                        mm.then_inc(s_wo, 1)
                        free[where] = (s_acc, n * WO_UNITS + i + 2)
                    elif kind == "xturn":
                        pe.wait_ge(*free[where])
                        x_transposed(unit_banks[where], b + 1, i)
                        free[where] = (s_xtlo, b * 4 + 4 + i + 1)

            def x_transposed(ps, b, g):
                pe.wait_ge(s_xn, b * NT + TPC * (g // 2 + 1))
                for r in range(TPC):
                    mm = pe.transpose(ps[:, r * P:(r + 1) * P], xn[:, TPC * (g // 2) + r, (g % 2) * P:(g % 2 + 1) * P], ident[:, :])
                mm.then_inc(s_xt, 1)

            pe.wait_ge(s_const, 2)
            for g in range(4):
                x_transposed(banks[4 + g], 0, g)
            with pe.Fori(0, B) as b:
                n0 = b * PAIRS
                pe.wait_ge(s_acc, n0 * WO_UNITS + 1)
                pe.wait_ge(s_flo, 1)
                for e in range(NC * IT):
                    c, i = e // IT, e % IT
                    if i == 0:
                        pe.wait_ge(s_xtlo, b * 4 + 2 * (c + 1))
                    if e >= 4:
                        pe.wait_ge(s_relu, b * 16 + e - 3)
                    for k in range(KT):
                        w = slice(i * P, (i + 1) * P)
                        mm = three(banks[e % 4], (up_hi[:, k, w], up_lo[:, k, w]), xT(k, c * CH, CH), k == 0, k == KT - 1)
                    mm.then_inc(s_up, 1)
                for t in range(NT):
                    c = t // TPC
                    toks = slice((t % TPC) * P, (t % TPC + 1) * P)
                    if t == 0:
                        pe.wait_ge(s_relu, b * 16 + 16)
                        pe.wait_ge(s_flo, 3)
                    if t >= 2:
                        pe.wait_ge(s_y, b * NT + t - 1)
                    for k in range(KT):
                        three(banks[2 + t % 2][:, 0:GW], xT(k, t * P, P), (eg_hi[:, k, :], eg_lo[:, k, :]), k == 0, k == KT - 1)
                    if t % TPC == 0:
                        pe.wait_ge(s_hlo, b * 16 + 8 * (c + 1))
                    for i in range(IT):
                        mm = three(banks[t % 2][:, 0:D], (hid_hi[c][:, i, toks], hid_lo[c][:, i, toks]),
                                   (down_hi[:, i, :], down_lo[:, i, :]), i == 0, i == IT - 1)
                    mm.then_inc(s_dn, 1)
                for kind, i in FIRST_ORDER:
                    if kind == "scores":
                        if i == 0:
                            pe.wait_ge(s_y, b * NT + NT)
                            pe.wait_ge(s_projlo, n0 * UNITS + 4)
                        if i >= 2:
                            pe.wait_ge(s_exp, n0 * TILES + i - 1)
                        scores(i)
                    elif kind == "proj":
                        if i in (0, 4, 8):
                            pe.wait_ge(s_wlo[i // 4], n0 + 2)
                        if i >= 4:
                            pe.wait_ge(s_projlo, n0 * UNITS + i - 3)
                        proj_products(banks[4 + i % 4], i)
                with pe.Fori(0, PAIRS - 1) as g:
                    step(b, b * PAIRS + g, False)
                step(b, b * PAIRS + PAIRS - 1, True)

        @block.scalar
        def _(act):
            def hi(dst, src, scale=1.0):
                return act.activation(dst, src, ACT.Copy, scale=scale)

            def weights_hi(n, part):
                act.wait_ge(s_raw[part], n * (32 if part <= PART_QK1 else 16) + (32 if part <= PART_QK1 else 16))
                hi(w_hi[:, part, :], w_raw[:, part, :]).then_inc(s_whi[part], 1)

            def proj_hi(ps, n, u):
                dst, _, is_q = proj_out(u)
                act.wait_ge(s_proj, n * UNITS + u + 1)
                hi(dst, ps, SCALE if is_q else 1.0).then_inc(s_projhi, 1)

            def exp(n, q):
                _, j, _, r, i = tile_of(q)
                w = (i + 1) * P
                act.wait_ge(s_max, n * TILES + q + 1)
                act.activation(prob[j][:, r, 0:w], ps_scores[q % 2][:, 0:w], ACT.Exp, bias=neg_max[:, q % TILES:q % TILES + 1],
                               accum_out=prob_sum[:, q % TILES:q % TILES + 1]).then_inc(s_exp, 1)

            def step(b, n, last):
                for kind, i, where in step_order(last):
                    if kind == "exp":
                        exp(n, i)
                    elif kind == "turn":
                        dst, _, at = turned(i)
                        act.wait_ge(s_pt, n * SLOTS + i + 1)
                        hi(dst, ps_turn[i % 2][:, at:CH]).then_inc(s_pthi, 1)
                    elif kind == "out":
                        act.wait_ge(s_pv, n * SLOTS + SLOT_BEGIN[i + 1])
                        hi(oT_hi[:, i // 2, (i % 2) * CH:(i % 2 + 1) * CH], ps_out[:, :]).then_inc(s_othi, 1)
                    elif kind == "weights":
                        if i == PART_O:
                            act.wait_ge(s_acc, n * WO_UNITS + 1)
                        weights_hi(n if i == PART_O else n + 1, i)
                    elif kind == "proj":
                        proj_hi(unit_banks[where], n + 1, i)
                    elif kind == "xturn":
                        x_hi(unit_banks[where], b + 1, i)

            def x_hi(ps, b, g):
                act.wait_ge(s_xt, b * 4 + g + 1)
                hi(xT_hi[:, g % 2, (g // 2) * CH:(g // 2 + 1) * CH], ps).then_inc(s_xthi, 1)

            act.wait_ge(s_fraw, 64)
            act.wait_ge(s_out, 32)
            hi(up_hi[:, :, :], up_raw).then_inc(s_fhi, 1)
            hi(down_hi[:, :, :], down_raw).then_inc(s_fhi, 1)
            hi(eg_hi[:, :, :], eg_raw).then_inc(s_fhi, 1)
            for g in range(4):
                x_hi(banks[4 + g], 0, g)
            act.wait_ge(s_flo, 3)
            with act.Fori(0, B) as b:
                n0 = b * PAIRS
                for part in (PART_QK0, PART_QK1, PART_V):
                    weights_hi(n0, part)

                def hidden_hi(e):
                    act.wait_ge(s_hid, b * 16 + e + 1)
                    hi(hid_hi[e // IT][:, e % IT, :], hid[:, e % IT, :]).then_inc(s_hhi, 1)

                for e in range(NC * IT):
                    if e >= IT:
                        act.wait_ge(s_hlo, b * 16 + e - IT + 1)
                    act.wait_ge(s_up, b * 16 + e + 1)
                    act.activation(hid[:, e % IT, :], banks[e % 4], ACT.Relu).then_inc(s_relu, 1)
                    if e > 0:
                        hidden_hi(e - 1)
                hidden_hi(NC * IT - 1)
                for kind, i in FIRST_ORDER:
                    if kind == "exp":
                        exp(n0, i)
                    elif kind == "proj":
                        proj_hi(banks[4 + i % 4], n0, i)
                with act.Fori(0, PAIRS - 1) as g:
                    step(b, b * PAIRS + g, False)
                step(b, b * PAIRS + PAIRS - 1, True)
                act.wait_ge(s_acc, b * PAIRS * WO_UNITS + PAIRS * WO_UNITS + 1)
                act.dma_start(out_v[b], acc[:, :, :]).then_inc(s_out, 16)
            act.wait_ge(s_out, 16 * B + 32)

        @block.vector
        def _(dve):
            def proj_lo(ps, n, u):
                h_, l_, is_q = proj_out(u)
                dve.wait_ge(s_projhi, n * UNITS + u + 1)
                if is_q:
                    ins = dve.scalar_tensor_tensor(out=l_, in0=ps, scalar=SCALE, in1=h_, op0=ALU.mult, op1=ALU.subtract)
                else:
                    ins = dve.tensor_tensor(l_, ps, h_, ALU.subtract)
                ins.then_inc(s_projlo, 1)

            def maximum(n, q):
                _, _, _, _, i = tile_of(q)
                dve.wait_ge(s_sc, n * TILES + q + 1)
                dve.tensor_reduce(neg_max[:, q % TILES:q % TILES + 1], ps_scores[q % 2][:, 0:(i + 1) * P], AX.X, ALU.max,
                                  negate=True).then_inc(s_max, 1)

            def step(b, n, last):
                for kind, i, where in step_order(last):
                    if kind == "scores":
                        maximum(n, i)
                    elif kind == "turn":
                        h_, l_, at = turned(i)
                        dve.wait_ge(s_pthi, n * SLOTS + i + 1)
                        dve.tensor_tensor(l_, ps_turn[i % 2][:, at:CH], h_, ALU.subtract).then_inc(s_ptlo, 1)
                    elif kind == "out":
                        cols = slice((i % 2) * CH, (i % 2 + 1) * CH)
                        dve.wait_ge(s_othi, n * HALVES + i + 1)
                        dve.tensor_tensor(oT_lo[:, i // 2, cols], ps_out[:, :], oT_hi[:, i // 2, cols], ALU.subtract).then_inc(s_otlo, 1)
                        four = slice(4 * i, 4 * i + 4)
                        dve.reciprocal(prob_rcp[:, four], prob_sum[:, four]).then_inc(s_rcp, 1)
                    elif kind == "proj":
                        proj_lo(unit_banks[where], n + 1, i)
                    elif kind == "wo":
                        dve.wait_ge(s_rcp, n * HALVES + i // 2 + 1)
                        dve.wait_ge(s_acc, n * WO_UNITS + (1 if i < 4 else i - 2))
                        dve.wait_ge(s_wo, n * WO_UNITS + i + 1)
                        for a, t in enumerate(wo_tiles(i)):
                            q = 4 * (i // 2) + t % 4
                            last_add = dve.scalar_tensor_tensor(out=acc[:, t, :], in0=unit_banks[where][:, a * D:(a + 1) * D],
                                                                scalar=prob_rcp[:, q:q + 1], in1=acc[:, t, :], op0=ALU.mult, op1=ALU.add)
                        last_add.then_inc(s_acc, 1)
                    elif kind == "moments":
                        if i == 0:
                            dve.wait_ge(s_xin, b * 16 + 32)
                        moments(b, xin, 0, NT, mean_x, rstd_x, i)
                    elif kind == "normed":
                        normed(i)
                    elif kind == "xturn":
                        x_lo(unit_banks[where], b + 1, i)

            dve.memset(ps_out[:, 0:1], 0.0).then_inc(s_otlo, 1)
            dve.memset(ps_proj[:, 0:1], 0.0).then_inc(s_acc, 1)
            dve.memset(pD_hi[:, 0:P].bitcast(F32), 0.0).then_inc(s_dve, 1)
            dve.memset(pD_lo[:, 0:P].bitcast(F32), 0.0).then_inc(s_dve, 1)

            before, done = 2 + MOMENTS, [2]

            def link(b, ins):
                done[0] += 1
                ins.then_inc(s_dve, 1)
                dve.wait_ge(s_dve, done[0] if b is None else b * CHAIN + before + done[0])

            def moments(b, src, lo, k, mean, rstd, part):
                ts = slice(lo, lo + k)
                st = stats[:, ts, :]
                if part < STATS:
                    first = lo + part * TPC // 2
                    tiles = [t for t in range(first, first + TPC // 2) if t < lo + k]
                    for t in tiles:
                        last = dve.bn_stats(stats[:, t, :], src[:, t, :])
                        if t == lo + k - 1:
                            link(b, last)
                elif part == STATS:
                    link(b, dve.tensor_tensor(tmp[:, ts], st[:, :, 1], st[:, :, 4], ALU.subtract))
                    dve.tensor_tensor(mean[:, ts], st[:, :, 1], st[:, :, 4], ALU.add)
                    dve.tensor_tensor(half[:, ts], st[:, :, 2], st[:, :, 5], ALU.add)
                    link(b, dve.scalar_tensor_tensor(out=var[:, ts], in0=tmp[:, ts], scalar=0.25, in1=tmp[:, ts], op0=ALU.mult, op1=ALU.mult))
                    link(b, dve.scalar_tensor_tensor(out=half[:, ts], in0=half[:, ts], scalar=1.0 / D, in1=var[:, ts], op0=ALU.mult, op1=ALU.add))
                    dve.tensor_scalar(mean[:, ts], mean[:, ts], 0.5, None, ALU.mult)
                    link(b, dve.tensor_scalar(var[:, ts], half[:, ts], EPS, None, ALU.add))
                elif part == STATS + 1:
                    link(b, dve.tensor_scalar(half[:, ts].bitcast(I32), var[:, ts].bitcast(I32), 1, None, ALU.logical_shift_right))
                    link(b, dve.tensor_scalar(rstd[:, ts].bitcast(I32), half[:, ts].bitcast(I32), -1.0, RSQRT_GUESS, ALU.mult, ALU.add))
                    link(b, dve.tensor_scalar(half[:, ts], var[:, ts], 0.5, None, ALU.mult))
                else:
                    link(b, dve.tensor_tensor(tmp[:, ts], rstd[:, ts], half[:, ts], ALU.mult))
                    link(b, dve.scalar_tensor_tensor(out=tmp[:, ts], in0=tmp[:, ts], scalar=-1.0, in1=rstd[:, ts], op0=ALU.mult, op1=ALU.mult))
                    link(b, dve.scalar_tensor_tensor(out=rstd[:, ts], in0=tmp[:, ts], scalar=1.5, in1=rstd[:, ts], op0=ALU.add, op1=ALU.mult))

            def normed(half_of_tiles):
                for t in range(TPC * half_of_tiles, TPC * (half_of_tiles + 1)):
                    dve.tensor_scalar(xn[:, t, :], xin[:, t, :], mean_x[:, t:t + 1], rstd_x[:, t:t + 1],
                                      ALU.subtract, ALU.mult).then_inc(s_xn, 1)

            def x_lo(ps, b, g):
                dst = slice((g // 2) * CH, (g // 2 + 1) * CH)
                dve.wait_ge(s_xthi, b * 4 + g + 1)
                dve.tensor_tensor(xT_lo[:, g % 2, dst], ps, xT_hi[:, g % 2, dst], ALU.subtract).then_inc(s_xtlo, 1)

            dve.wait_ge(s_xin, 16)
            for part in range(MOMENT_PARTS):
                moments(None, xin, 0, NT, mean_x, rstd_x, part)
            normed(0)
            normed(1)
            for g in range(4):
                x_lo(banks[4 + g], 0, g)
            with dve.Fori(0, B) as b:
                n0 = b * PAIRS
                done[0] = 0

                def feed_forward_sum(t):
                    dve.wait_ge(s_dn, b * NT + t + 1)
                    dve.tensor_copy(y[:, t, :], banks[t % 2][:, 0:D])
                    link(b, dve.max(top8[:, t, :], banks[2 + t % 2][:, D:GW]))
                    link(b, dve.tensor_tensor(top2[:, t:t + 1], top8[:, t, 0:1], top8[:, t, 1:2], ALU.add))
                    dve.scalar_tensor_tensor(out=y[:, t, :], in0=banks[2 + t % 2][:, 0:D], scalar=top2[:, t:t + 1], in1=y[:, t, :],
                                             op0=ALU.mult, op1=ALU.add).then_inc(s_y, 1)

                def normed_y(c):
                    for t in range(TPC * c, TPC * (c + 1)):
                        dve.tensor_scalar(y[:, t, :], y[:, t, :], mean[:, t:t + 1], rstd[:, t:t + 1],
                                          ALU.subtract, ALU.mult).then_inc(s_yn, 1)

                def hidden_lo(e):
                    dve.wait_ge(s_hhi, b * 16 + e + 1)
                    dve.tensor_tensor(hid_lo[e // IT][:, e % IT, :], hid[:, e % IT, :], hid_hi[e // IT][:, e % IT, :],
                                      ALU.subtract).then_inc(s_hlo, 1)

                for e in range(NC * IT):
                    dve.wait_ge(s_relu, b * 16 + e + 1)
                    r = hid[:, e % IT, :]
                    dve.tensor_tensor(r, r, r, ALU.mult).then_inc(s_hid, 1)
                    if e > 0:
                        hidden_lo(e - 1)
                hidden_lo(NC * IT - 1)
                for t in range(NT):
                    feed_forward_sum(t)
                    if t == TPC - 1 or t == NT - 1:
                        dve.wait_ge(s_y, b * NT + t + 1)
                    for part in {3: (0, 1), 4: (4, 5), 5: (6,), 6: (7, 8)}.get(t, ()):
                        moments(b, y, 0, TPC, mean, rstd, part)
                    if t == 6:
                        normed_y(0)
                for kind, i in FIRST_ORDER:
                    if kind == "scores":
                        maximum(n0, i)
                    elif kind == "proj":
                        proj_lo(banks[4 + i % 4], n0, i)
                    elif kind == "moments":
                        moments(b, y, TPC, TPC, mean, rstd, i)
                    elif kind == "normed":
                        normed_y(i)
                with dve.Fori(0, PAIRS - 1) as g:
                    step(b, b * PAIRS + g, False)
                step(b, b * PAIRS + PAIRS - 1, True)
                assert done[0] == CHAIN


_INS = ["L0_attn_hidden_states", "L0_attn_Wq", "L0_attn_Wk", "L0_attn_Wv", "L0_attn_Wo", "L0_ffn_gate_w",
        "L0_ffn_up_w", "L0_ffn_down_w", "L0_ffn_expert_weight", "L0_ffn_ln_gamma", "L0_ffn_ln_beta"]


def kernel(**inputs):
    import numpy as _np
    import concourse.bacc as _bacc
    from concourse import mybir as _mybir
    from concourse.bass_utils import run_bass_kernel_spmd as _run

    nc = _bacc.Bacc("TRN2", target_bir_lowering=False, num_devices=1)
    arrays, args = {}, []
    for name in _INS:
        a = _np.ascontiguousarray(inputs[name])
        arrays[f"in_{name}_dram"] = a
        args.append(nc.dram_tensor(f"in_{name}_dram", a.shape, _mybir.dt.from_np(a.dtype), kind="ExternalInput").ap())
    shape = inputs[_INS[0]].shape
    out = nc.dram_tensor("out_0_dram", shape, _mybir.dt.float32, kind="ExternalOutput").ap()
    layer_kernel(nc, *args, out)
    r = _run(nc, [arrays], core_ids=[0])
    return r.results[0]["out_0_dram"]
```

```python
from contextlib import ExitStack

import concourse.bass as bass
from concourse import mybir

F32 = mybir.dt.float32
F32R = mybir.dt.float32r
I32 = mybir.dt.int32
ALU = mybir.AluOpType
ACT = mybir.ActivationFunctionType
AX = mybir.AxisListType

P = 128
EPS = 1e-5
MASKED = -1e30
RSQRT_GUESS = float(0x5F3759DF)
NEWTON = 3

TILES = 16
SLOTS = 24
UNITS = 12
HALVES = 4
WO_UNITS = 8
PARTS = 4
SLOT_BEGIN = [0, 4, 12, 16, 24]
PART_QK0, PART_QK1, PART_V, PART_O = range(4)


PROJ_BANK, SPARE0, SPARE1, TURN1 = range(4)
SPARES = (SPARE0, SPARE1)


STEP_ORDER = [
    ("turn", 0, None), ("scores", 4, None), ("scores", 5, None), ("turn", 1, None), ("exp", 4, None),
    ("turn", 2, None), ("exp", 5, None), ("weights", PART_QK0, None), ("pv", 0, None), ("scores", 6, None),
    ("turn", 3, None), ("exp", 6, None), ("scores", 7, None), ("exp", 7, None), ("pv", 1, None), ("pv", 2, None),
    ("proj", 0, PROJ_BANK), ("proj", 1, SPARE0), ("scores", 8, None), ("turn", 4, None), ("pv", 3, None),
    ("out", 0, None), ("weights", PART_O, None), ("turn", 5, None), ("proj", 2, SPARE1), ("turn", 6, None),
    ("scores", 9, None), ("exp", 8, None), ("pv", 4, None), ("turn", 7, None), ("exp", 9, None), ("pv", 5, None),
    ("scores", 10, None), ("turn", 8, None), ("exp", 10, None), ("weights", PART_QK1, None), ("pv", 6, None),
    ("wo", 0, PROJ_BANK), ("turn", 9, None), ("pv", 7, None), ("scores", 11, None), ("turn", 10, None),
    ("exp", 11, None), ("pv", 8, None), ("wo", 1, SPARE0), ("weights", PART_V, None), ("turn", 11, None),
    ("pv", 9, None), ("proj", 3, SPARE1), ("turn", 12, None), ("pv", 10, None), ("pv", 11, None), ("out", 1, None),
    ("scores", 12, None), ("scores", 13, None), ("exp", 12, None), ("turn", 13, None), ("pv", 12, None),
    ("turn", 14, None), ("exp", 13, None), ("wo", 2, PROJ_BANK), ("scores", 14, None), ("exp", 14, None),
    ("pv", 13, None), ("scores", 15, None), ("proj", 4, PROJ_BANK), ("exp", 15, None), ("turn", 15, None),
    ("pv", 14, None), ("proj", 5, SPARE0), ("wo", 3, PROJ_BANK), ("turn", 16, None), ("pv", 15, None),
    ("out", 2, None), ("scores", 16, None), ("turn", 17, None), ("proj", 6, SPARE1), ("turn", 18, None),
    ("exp", 16, None), ("pv", 16, None), ("scores", 17, None), ("turn", 19, None), ("exp", 17, None),
    ("scores", 18, None), ("pv", 17, None), ("wo", 4, PROJ_BANK), ("turn", 20, None), ("exp", 18, None),
    ("pv", 18, None), ("scores", 19, None), ("turn", 21, None), ("exp", 19, None), ("pv", 19, None),
    ("wo", 5, SPARE0), ("turn", 22, None), ("pv", 20, None), ("proj", 7, PROJ_BANK), ("turn", 23, None),
    ("pv", 21, None), ("proj", 8, SPARE1), ("pv", 22, None), ("pv", 23, None), ("proj", 9, PROJ_BANK),
    ("out", 3, None), ("proj", 10, SPARE0), ("proj", 11, SPARE1), ("wo", 6, PROJ_BANK), ("wo", 7, TURN1),
]
LAST_STEP_ORDER = [
    ("turn", 0, None), ("scores", 4, None), ("scores", 5, None), ("exp", 4, None), ("turn", 1, None),
    ("turn", 2, None), ("pv", 0, None), ("exp", 5, None), ("scores", 6, None), ("xturn", 0, PROJ_BANK),
    ("exp", 6, None), ("scores", 7, None), ("pv", 1, None), ("xturn", 1, PROJ_BANK), ("exp", 7, None),
    ("turn", 3, None), ("pv", 2, None), ("expert", 0, PROJ_BANK), ("weights", PART_O, None), ("turn", 4, None),
    ("expert", 1, SPARE0), ("pv", 3, None), ("out", 0, None), ("xturn", 2, SPARE1), ("turn", 5, None),
    ("scores", 8, None), ("xturn", 3, PROJ_BANK), ("turn", 6, None), ("exp", 8, None), ("pv", 4, None),
    ("scores", 9, None), ("turn", 7, None), ("pv", 5, None), ("scores", 10, None), ("turn", 8, None),
    ("exp", 9, None), ("exp", 10, None), ("pv", 6, None), ("wo", 0, PROJ_BANK), ("turn", 9, None),
    ("scores", 11, None), ("pv", 7, None), ("turn", 10, None), ("exp", 11, None), ("pv", 8, None), ("wo", 1, SPARE0),
    ("turn", 11, None), ("pv", 9, None), ("expert", 2, SPARE1), ("pv", 10, None), ("scores", 12, None),
    ("turn", 12, None), ("pv", 11, None), ("out", 1, None), ("scores", 13, None), ("exp", 12, None),
    ("turn", 13, None), ("turn", 14, None), ("exp", 13, None), ("pv", 12, None), ("scores", 14, None),
    ("wo", 2, PROJ_BANK), ("exp", 14, None), ("scores", 15, None), ("pv", 13, None), ("expert", 3, PROJ_BANK),
    ("turn", 15, None), ("exp", 15, None), ("pv", 14, None), ("expert", 4, SPARE0), ("wo", 3, PROJ_BANK),
    ("turn", 16, None), ("pv", 15, None), ("expert", 5, SPARE1), ("out", 2, None), ("turn", 17, None),
    ("turn", 18, None), ("pv", 16, None), ("turn", 19, None), ("pv", 17, None), ("wo", 4, SPARE1), ("turn", 20, None),
    ("pv", 18, None), ("turn", 21, None), ("wo", 5, SPARE1), ("pv", 19, None), ("turn", 22, None), ("pv", 20, None),
    ("turn", 23, None), ("pv", 21, None), ("pv", 22, None), ("pv", 23, None), ("out", 3, None), ("expert", 6, SPARE0),
    ("expert", 7, SPARE1), ("wo", 6, PROJ_BANK), ("wo", 7, TURN1),
]


def step_order(last):
    return LAST_STEP_ORDER if last else STEP_ORDER


FIRST_ORDER = [("proj", 0), ("stats", 3), ("proj", 1), ("proj", 2), ("proj", 3), ("proj", 4),
               ("scores", 0), ("exp", 0), ("proj", 5), ("scores", 1), ("exp", 1), ("proj", 6),
               ("scores", 2), ("exp", 2), ("proj", 7), ("scores", 3), ("exp", 3),
               ("proj", 8), ("proj", 9), ("proj", 10), ("normed", 1), ("proj", 11)]


def layer_kernel(nc, x, wq, wk, wv, wo, gate_w, up_w, down_w, expert_w, gamma, beta, out):
    B, S, D = x.shape
    HEADS_D = wq.shape[1]
    INTER = up_w.shape[1]
    EXPERTS = gate_w.shape[1]
    KT = D // P
    NT = S // P
    CH = 512
    NC = S // CH
    TPC = CH // P
    IT = INTER // P
    PAIRS = HEADS_D // (2 * P)
    SCALE = float(P) ** -0.5
    GW = D + EXPERTS
    assert (D, S, KT, NT, NC, IT) == (256, 1024, 2, 8, 2, 8)

    x_v = x.rearrange("b (t p) d -> b p t d", p=P)
    out_v = out.rearrange("b (t p) d -> b p t d", p=P)
    wq_v = wq.rearrange("(k p) (g s c) -> g s p k c", p=P, s=2, c=P)
    wk_v = wk.rearrange("(k p) (g s c) -> g s p k c", p=P, s=2, c=P)
    wv_v = wv.rearrange("(k p) (g c) -> g p k c", p=P, c=2 * P)
    wo_v = wo.rearrange("(g s p) n -> g p s n", p=P, s=2)

    with ExitStack() as ctx:
        def sb(name, shape, dt=F32):
            return ctx.enter_context(nc.sbuf_tensor(name, shape, dt))

        def bank(name, n=1):
            return ctx.enter_context(nc.psum_tensor(name, [P, 512 * n], F32))

        def sem(name):
            return ctx.enter_context(nc.semaphore(name))

        xT_hi, xT_lo = (sb(f"xT_{h}", [P, KT, S], F32R) for h in ("hi", "lo"))
        shared = sb("shared", [P, 16384], F32R)
        qk_hi = shared[:, 0:4096].rearrange("p (h m s) -> p h m s", h=2, m=2)
        qk_lo = shared[:, 4096:8192].rearrange("p (h m s) -> p h m s", h=2, m=2)
        v_hi = shared[:, 8192:10240].rearrange("p (t h c) -> p t h c", t=NT, h=2)
        v_lo = shared[:, 10240:12288].rearrange("p (t h c) -> p t h c", t=NT, h=2)
        oT_hi = shared[:, 12288:14336].rearrange("p (h s) -> p h s", h=2)
        oT_lo = shared[:, 14336:16384].rearrange("p (h s) -> p h s", h=2)
        hid_hi = [shared[:, 8192 * c:8192 * c + 4096].rearrange("p (i s) -> p i s", i=IT) for c in range(NC)]
        hid_lo = [shared[:, 8192 * c + 4096:8192 * c + 8192].rearrange("p (i s) -> p i s", i=IT) for c in range(NC)]
        prob = [sb("prob0", [P, TPC, CH]), sb("prob1", [P, TPC, S])]
        hid = prob[1][:, :, :].rearrange("p r (a s) -> p (r a) s", a=2)
        pT_hi, pT_lo = (sb(f"pT_{h}", [P, 3, CH], F32R) for h in ("hi", "lo"))
        pD_hi, pD_lo = (sb(f"pD_{h}", [P, 2 * P], F32R) for h in ("hi", "lo"))
        w_raw = sb("w_raw", [P, PARTS, 512])
        w_hi, w_lo = (sb(f"w_{h}", [P, PARTS, 512], F32R) for h in ("hi", "lo"))
        up_hi, up_lo = (sb(f"up_{h}", [P, KT, INTER], F32R) for h in ("hi", "lo"))
        down_hi, down_lo = (sb(f"down_{h}", [P, IT, D], F32R) for h in ("hi", "lo"))
        eg_hi, eg_lo = (sb(f"eg_{h}", [P, KT, GW], F32R) for h in ("hi", "lo"))
        up_raw = prob[1][:, 0:2, :]
        down_raw = prob[1][:, 2:4, :].rearrange("p r (a n) -> p (r a) n", n=D)
        acc = sb("acc", [P, NT, D])
        eg_raw = acc[:, :, :].rearrange("p t d -> p (t d)")[:, 0:KT * GW].rearrange("p (k n) -> p k n", k=KT)
        xin = sb("xin", [P, NT, D])
        y = sb("y", [P, NT, D])
        gamma_b, beta_b = sb("gamma_b", [P, D]), sb("beta_b", [P, D])
        ident = sb("ident", [P, P])
        mask = sb("mask", [P, P])
        stats, stats_x = sb("stats", [P, NT, 6]), sb("stats_x", [P, NT, 6])
        mean, var, rstd, tmp, half = (sb(n, [P, NT]) for n in ("mean", "var", "rstd", "tmp", "half"))
        halves, three_halves = sb("halves", [P, NT]), sb("three_halves", [P, NT])
        mean_x, rstd_x = sb("mean_x", [P, NT]), sb("rstd_x", [P, NT])
        top8 = sb("top8", [P, NT, 8])
        top2 = sb("top2", [P, NT])
        neg_max, prob_sum, prob_rcp = (sb(n, [P, TILES]) for n in ("neg_max", "prob_sum", "prob_rcp"))

        ps_scores = [bank("ps_scores0", 2), bank("ps_scores1", 2)]
        ps_turn = [bank("ps_turn0"), bank("ps_turn1")]
        ps_out, ps_proj = bank("ps_out"), bank("ps_proj")
        banks = [ps_scores[0][:, 0:512], ps_scores[0][:, 512:1024], ps_scores[1][:, 0:512],
                 ps_scores[1][:, 512:1024], ps_turn[0][:, :], ps_turn[1][:, :], ps_out[:, :], ps_proj[:, :]]

        unit_banks = [banks[7], banks[1], banks[3], banks[5]]

        s_const = sem("constants_made")
        s_upraw, s_downraw, s_gamma = sem("up_loaded"), sem("down_loaded"), sem("gamma_beta_loaded")
        s_fhi, s_flo = sem("ffn_weights_hi"), sem("ffn_weights_lo")
        s_xin = sem("x_loaded")
        s_raw = [sem(f"weights_loaded{p}") for p in range(PARTS)]
        s_whi, s_wlo = ([sem(f"weights_{h}{p}") for p in range(PARTS)] for h in ("hi", "lo"))
        s_dve = sem("vector_chain")
        s_xn, s_xt, s_xthi, s_xtlo = sem("xn_made"), sem("xT_made"), sem("xT_hi_made"), sem("xT_lo_made")
        s_up, s_relu, s_hid, s_hhi, s_hlo = sem("up_done"), sem("relu_made"), sem("hid_made"), sem("hid_hi_made"), sem("hid_lo_made")
        s_eg, s_egread = sem("expert_done"), sem("expert_read")
        s_dn, s_top2, s_y, s_yn = sem("down_done"), sem("top2_made"), sem("y_made"), sem("y_normed")
        s_stats, s_moments = sem("statistics_made"), sem("moments_made")
        s_pool, s_fin = sem("pool_chain"), sem("ffn_added")
        s_proj, s_projhi, s_projlo = sem("proj_done"), sem("proj_hi_made"), sem("proj_lo_made")
        s_masked = sem("diagonal_masked")
        s_sc, s_max, s_exp, s_rcp = (sem(n) for n in ("scores_done", "max_made", "exp_made", "rcp_made"))
        s_pt, s_pthi, s_ptlo, s_pv = sem("turned"), sem("pT_hi_made"), sem("pT_lo_made"), sem("pv_done")
        s_othi, s_otlo = sem("oT_hi_made"), sem("oT_lo_made")
        s_accx = sem("acc_is_x")
        s_wo, s_acc, s_out = sem("wo_done"), sem("acc_added"), sem("expert_loaded_acc_stored")

        MOMENTS = 4 + 4 * NEWTON
        POOL_CHAIN = 3 * MOMENTS + NT + 1

        def tile_of(q):
            h = q // 4
            return h, h % 2, (h // 2) % 2, q % 4, 4 * (h % 2) + q % 4

        def slot_of(s):
            h = max(i for i in range(HALVES) if SLOT_BEGIN[i] <= s)
            j, kt = h % 2, s - SLOT_BEGIN[h]
            return h, j, h // 2, kt, max(0, kt - 4 * j)

        def proj_out(u):
            if u < 8:
                h, m, c = u // 4, (u % 4) // 2, u % 2
                return qk_hi[:, h, m, c * CH:(c + 1) * CH], qk_lo[:, h, m, c * CH:(c + 1) * CH], m == 0
            t = 2 * (u - 8)
            flat = "p t h c -> p (t h c)"
            return v_hi[:, t:t + 2].rearrange(flat), v_lo[:, t:t + 2].rearrange(flat), False

        def wo_tiles(i):
            t = 4 * (i // 2 % 2) + 2 * (i % 2)
            return t, t + 1

        def turned(s):
            _, _, _, _, r = slot_of(s)
            if r == TPC - 1:
                return pD_hi[:, P:2 * P], pD_lo[:, P:2 * P], r * P
            return pT_hi[:, s % 3, r * P:CH], pT_lo[:, s % 3, r * P:CH], r * P

        block = ctx.enter_context(nc.Block())

        @block.sync
        def _(sp):
            sp.dma_start(xin[:, :, :], x_v[0]).then_inc(s_xin, 16)
            sp.dma_start(eg_raw[:, :, 0:D], expert_w.rearrange("(k p) n -> p k n", p=P)).then_inc(s_out, 16)
            with nc.allow_non_contiguous_dma(reason="rows of 8 gate weights"):
                sp.dma_start(eg_raw[:, :, D:GW], gate_w.rearrange("(k p) n -> p k n", p=P)).then_inc(s_out, 16)
            sp.dma_start(up_raw, up_w.rearrange("(k p) n -> p k n", p=P)).then_inc(s_upraw, 16)
            sp.dma_start(down_raw, down_w.rearrange("(k p) n -> p k n", p=P)).then_inc(s_downraw, 16)
            sp.dma_start(gamma_b[:, :], gamma.rearrange("(a d) -> a d", a=1).broadcast_to([P, D])).then_inc(s_gamma, 16)
            sp.dma_start(beta_b[:, :], beta.rearrange("(a d) -> a d", a=1).broadcast_to([P, D])).then_inc(s_gamma, 16)
            sp.wait_ge(s_xt, 4)
            sp.dma_start(xin[:, :, :], x_v[1 % B]).then_inc(s_xin, 16)
            with sp.Fori(0, B) as b:
                with sp.Fori(0, PAIRS) as g:
                    n = b * PAIRS + g
                    for h, part in ((0, PART_QK0), (1, PART_QK1)):
                        raw = w_raw[:, part, :].rearrange("p (m k c) -> p m k c", m=2, k=KT)
                        sp.wait_ge(s_wlo[part], n + 1)
                        sp.dma_start(raw[:, 0], wq_v[g, h]).then_inc(s_raw[part], 16)
                        sp.dma_start(raw[:, 1], wk_v[g, h]).then_inc(s_raw[part], 16)
                    sp.wait_ge(s_wlo[PART_V], n + 1)
                    sp.dma_start(w_raw[:, PART_V, :].rearrange("p (k c) -> p k c", k=KT), wv_v[g]).then_inc(s_raw[PART_V], 16)
                    sp.wait_ge(s_wlo[PART_O], n + 1)
                    sp.dma_start(w_raw[:, PART_O, :].rearrange("p (s c) -> p s c", s=2), wo_v[g]).then_inc(s_raw[PART_O], 16)
                sp.wait_ge(s_xt, b * 4 + 8)
                sp.dma_start(xin[:, :, :], x_v[(b + 2) % B]).then_inc(s_xin, 16)
            sp.wait_ge(s_xin, 16 * B + 32)

        @block.gpsimd
        def _(pool):
            for part in range(PARTS):
                pool.memset(w_raw[:, part, 0:1], 0.0).then_inc(s_wlo[part], 1)
            pool.memset(ident[:, :], 0.0).then_inc(s_pool, 1)
            pool.memset(mask[:, :], 0.0).then_inc(s_pool, 1)
            pool.memset(halves[:, :], 0.5)
            pool.memset(three_halves[:, :], 1.5)
            pool.wait_ge(s_pool, 2)
            pool.affine_select(out=ident[:, :], in_=ident[:, :], compare_op=ALU.not_equal, fill=1.0, base=0,
                               pattern=[[-1, P]], channel_multiplier=1).then_inc(s_const, 1)
            pool.affine_select(out=mask[:, :], in_=mask[:, :], compare_op=ALU.is_ge, fill=MASKED, base=0,
                               pattern=[[-1, P]], channel_multiplier=1).then_inc(s_const, 1)

            def split_lo(n, part):
                pool.wait_ge(s_whi[part], n + 1)
                pool.tensor_tensor(w_lo[:, part, :], w_raw[:, part, :], w_hi[:, part, :], ALU.subtract).then_inc(s_wlo[part], 1)

            before, done = 2 + MOMENTS, [2]

            def link(b, ins):
                done[0] += 1
                ins.then_inc(s_pool, 1)
                pool.wait_ge(s_pool, done[0] if b is None else b * POOL_CHAIN + before + done[0])

            def moments(b, stats, lo, k, mean, rstd):
                ts = slice(lo, lo + k)
                st = stats[:, ts, :]
                link(b, pool.tensor_tensor(tmp[:, ts], st[:, :, 1], st[:, :, 4], ALU.subtract))
                pool.tensor_tensor(mean[:, ts], st[:, :, 1], st[:, :, 4], ALU.add)
                pool.tensor_tensor(half[:, ts], st[:, :, 2], st[:, :, 5], ALU.add)
                link(b, pool.tensor_scalar(tmp[:, ts], tmp[:, ts], 0.5, None, ALU.mult))
                pool.tensor_tensor(tmp[:, ts], tmp[:, ts], tmp[:, ts], ALU.mult)
                pool.tensor_scalar(mean[:, ts], mean[:, ts], 0.5, None, ALU.mult)
                link(b, pool.tensor_scalar(half[:, ts], half[:, ts], 1.0 / D, EPS, ALU.mult, ALU.add))
                link(b, pool.tensor_tensor(var[:, ts], half[:, ts], tmp[:, ts], ALU.add))
                pool.tensor_tensor(half[:, ts], var[:, ts], halves[:, ts], ALU.mult)
                link(b, pool.tensor_scalar(rstd[:, ts].bitcast(I32), var[:, ts].bitcast(I32), -0.5, RSQRT_GUESS, ALU.mult, ALU.add))
                for i in range(NEWTON):
                    link(b, pool.tensor_tensor(tmp[:, ts], rstd[:, ts], half[:, ts], ALU.mult))
                    link(b, pool.tensor_tensor(tmp[:, ts], tmp[:, ts], rstd[:, ts], ALU.mult))
                    link(b, pool.tensor_tensor(tmp[:, ts], three_halves[:, ts], tmp[:, ts], ALU.subtract))
                    ins = pool.tensor_tensor(rstd[:, ts], rstd[:, ts], tmp[:, ts], ALU.mult)
                    if i < NEWTON - 1:
                        link(b, ins)
                ins.then_inc(s_moments, 1)

            pool.wait_ge(s_stats, 1)
            moments(None, stats_x, 0, NT, mean_x, rstd_x)
            pool.wait_ge(s_gamma, 32)
            pool.wait_ge(s_flo, 1)
            with pool.Fori(0, B) as b:
                for part in (PART_QK0, PART_QK1, PART_V):
                    split_lo(b * PAIRS, part)
                done[0] = 0
                pool.wait_ge(s_out, b * 16 + 32)
                pool.dma_start(acc[:, :, :], x_v[b]).then_inc(s_accx, 16)
                done[0] = 0
                pool.wait_ge(s_stats, b * 3 + 2)
                moments(b, stats_x, 0, NT, mean_x, rstd_x)
                for t in range(NT):
                    if t % TPC == 0:
                        pool.wait_ge(s_moments, b * 3 + 2 + t // TPC)
                        pool.wait_ge(s_stats, b * 3 + 3 + t // TPC)
                        moments(b, stats, t, TPC, mean, rstd)
                    if t == 0:
                        pool.wait_ge(s_accx, b * 16 + 16)
                        for a in range(NT):
                            ins = pool.tensor_tensor(acc[:, a, :], acc[:, a, :], beta_b[:, :], ALU.add)
                        link(b, ins)
                    pool.wait_ge(s_yn, b * NT + t + 1)
                    link(b, pool.tensor_tensor(y[:, t, :], y[:, t, :], gamma_b[:, :], ALU.mult))
                    pool.tensor_tensor(acc[:, t, :], y[:, t, :], acc[:, t, :], ALU.add).then_inc(s_fin, 1)
                assert done[0] == POOL_CHAIN
                with pool.Fori(0, PAIRS - 1) as g:
                    n = b * PAIRS + g
                    split_lo(n + 1, PART_QK0)
                    split_lo(n, PART_O)
                    split_lo(n + 1, PART_QK1)
                    split_lo(n + 1, PART_V)
                split_lo(b * PAIRS + PAIRS - 1, PART_O)

        @block.tensor
        def _(pe):
            def three(ps, w_parts, m_parts, first, final):
                for i, (a, c) in enumerate(((0, 1), (1, 0), (0, 0))):
                    mm = pe.matmul(ps, w_parts[a], m_parts[c], start=first and i == 0, stop=final and i == 2)
                return mm

            def xT(k, lo, n):
                return xT_hi[:, k, lo:lo + n], xT_lo[:, k, lo:lo + n]

            def proj_products(ps, u):
                if u < 8:
                    h, m, c = u // 4, (u % 4) // 2, u % 2
                    part = (PART_QK0, PART_QK1)[h]
                    for k in range(KT):
                        at = (m * KT + k) * P
                        mm = three(ps, (w_hi[:, part, at:at + P], w_lo[:, part, at:at + P]), xT(k, c * CH, CH), k == 0, k == KT - 1)
                else:
                    for a in range(2):
                        for k in range(KT):
                            w = slice(k * 2 * P, (k + 1) * 2 * P)
                            mm = three(ps[:, a * 256:(a + 1) * 256], xT(k, (2 * (u - 8) + a) * P, P),
                                       (w_hi[:, PART_V, w], w_lo[:, PART_V, w]), k == 0, k == KT - 1)
                mm.then_inc(s_proj, 1)

            def scores(q):
                _, j, h, _, i = tile_of(q)
                width = (i + 1) * P
                ps = ps_scores[q % 2]
                qs = slice(i * P, (i + 1) * P)
                for c in range(j + 1):
                    w = min(CH, max(width - c * CH, 2 * P))
                    ks = slice(c * CH, c * CH + w)
                    mm = three(ps[:, ks], (qk_hi[:, h, 0, qs], qk_lo[:, h, 0, qs]), (qk_hi[:, h, 1, ks], qk_lo[:, h, 1, ks]), True, True)
                mm.then_inc(s_sc, 1)

            def step(b, n, last):
                free = {PROJ_BANK: (s_acc, n * WO_UNITS + 1), SPARE0: (s_projlo, n * UNITS + UNITS - 1), SPARE1: (s_projlo, n * UNITS + UNITS),
                        TURN1: (s_ptlo, n * SLOTS + SLOTS)}
                for kind, i, where in step_order(last):
                    if kind == "scores":
                        if i == 8:
                            pe.wait_ge(s_projlo, n * UNITS + 8)
                        if i == 16:
                            pe.wait_ge(s_projlo, n * UNITS + UNITS + 4)
                        pe.wait_ge(s_exp, n * TILES + i - 1)
                        if tile_of(i)[1] == 1:
                            pe.wait_ge(*free[SPARES[i % 2]])
                            free[SPARES[i % 2]] = (s_exp, n * TILES + i + 1)
                        scores(i)
                    elif kind == "turn":
                        h, j, _, kt, r0 = slot_of(i)
                        if i == 0:
                            pe.wait_ge(s_projlo, n * UNITS + 10)
                        if i == 1:
                            pe.wait_ge(s_acc, n * WO_UNITS + 1)
                        if kt == 0:
                            pe.wait_ge(s_exp, n * TILES + 4 * (h + 1))
                        if i >= 2:
                            pe.wait_ge(s_ptlo, n * SLOTS + i - 1)
                        for r in range(r0, TPC):
                            mm = pe.transpose(ps_turn[i % 2][:, r * P:(r + 1) * P], prob[j][:, r, kt * P:(kt + 1) * P], ident[:, :])
                        mm.then_inc(s_pt, 1)
                    elif kind == "pv":
                        h, j, hd, kt, r0 = slot_of(i)
                        if i == 0:
                            pe.wait_ge(s_projlo, n * UNITS + UNITS)
                        if kt == 0:
                            pe.wait_ge(s_otlo, n * HALVES + h + 1)
                        pe.wait_ge(s_ptlo, n * SLOTS + i + 1)
                        if r0 == TPC - 1:
                            m, cols = (pD_hi[:, :], pD_lo[:, :]), slice(CH - 2 * P, CH)
                        else:
                            m, cols = (pT_hi[:, i % 3, r0 * P:CH], pT_lo[:, i % 3, r0 * P:CH]), slice(r0 * P, CH)
                        three(ps_out[:, cols], (v_hi[:, kt, hd, :], v_lo[:, kt, hd, :]), m, kt == 0,
                              kt == 4 * j + 3).then_inc(s_pv, 1)
                    elif kind == "proj":
                        pe.wait_ge(*free[where])
                        if i in (0, 4, 8):
                            pe.wait_ge(s_wlo[(PART_QK0, PART_QK1, PART_V)[i // 4]], n + 3)
                        proj_products(unit_banks[where], i)
                        free[where] = (s_projlo, n * UNITS + UNITS + i + 1)
                    elif kind == "wo":
                        h, w = i // 4, slice(i // 4 * D, (i // 4 + 1) * D)
                        pe.wait_ge(*free[where])
                        if i == 0:
                            pe.wait_ge(s_wlo[PART_O], n + 2)
                        pe.wait_ge(s_otlo, n * HALVES + i // 2 + 2)
                        for a, t in enumerate(wo_tiles(i)):
                            mm = three(unit_banks[where][:, a * D:(a + 1) * D], (oT_hi[:, h, t * P:(t + 1) * P], oT_lo[:, h, t * P:(t + 1) * P]),
                                       (w_hi[:, PART_O, w], w_lo[:, PART_O, w]), True, True)
                        mm.then_inc(s_wo, 1)
                        free[where] = (s_acc, n * WO_UNITS + i + 2)
                    elif kind == "xturn":
                        pe.wait_ge(*free[where])
                        x_transposed(unit_banks[where], b + 1, i)
                        free[where] = (s_xtlo, b * 4 + 4 + i + 1)
                    elif kind == "expert":
                        pe.wait_ge(*free[where])
                        expert_products(unit_banks[where], b + 1, i)
                        free[where] = (s_egread, b * NT + NT + i + 1)

            def x_transposed(ps, b, g):
                pe.wait_ge(s_xn, b * NT + TPC * (g // 2 + 1))
                for r in range(TPC):
                    mm = pe.transpose(ps[:, r * P:(r + 1) * P], xin[:, TPC * (g // 2) + r, (g % 2) * P:(g % 2 + 1) * P], ident[:, :])
                mm.then_inc(s_xt, 1)

            def expert_products(ps, b, t):
                pe.wait_ge(s_xtlo, b * 4 + 2 * (t // TPC) + 2)
                for k in range(KT):
                    mm = three(ps[:, 0:GW], xT(k, t * P, P), (eg_hi[:, k, :], eg_lo[:, k, :]), k == 0, k == KT - 1)
                mm.then_inc(s_eg, 1)

            pe.wait_ge(s_const, 2)
            for g in range(4):
                x_transposed(banks[4 + g], 0, g)
            pe.wait_ge(s_flo, 1)
            for t in range(NT):
                if t >= 4:
                    pe.wait_ge(s_egread, t - 3)
                expert_products(banks[t % 4], 0, t)
            with pe.Fori(0, B) as b:
                n0 = b * PAIRS
                pe.wait_ge(s_flo, 2)
                for e in range(NC * IT):
                    c, i = e // IT, e % IT
                    if e == 0:
                        pe.wait_ge(s_egread, b * NT + 5)
                    if e == 1:
                        pe.wait_ge(s_egread, b * NT + NT)
                    if e == 3:
                        pe.wait_ge(s_acc, n0 * WO_UNITS + 1)
                    if e >= 4:
                        pe.wait_ge(s_relu, b * 16 + e - 3)
                    for k in range(KT):
                        w = slice(i * P, (i + 1) * P)
                        mm = three(banks[e % 4], (up_hi[:, k, w], up_lo[:, k, w]), xT(k, c * CH, CH), k == 0, k == KT - 1)
                    mm.then_inc(s_up, 1)
                pe.wait_ge(s_flo, 3)
                for t in range(NT):
                    c = t // TPC
                    toks = slice((t % TPC) * P, (t % TPC + 1) * P)
                    if t < 4:
                        pe.wait_ge(s_relu, b * 16 + 13 + t)
                    else:
                        pe.wait_ge(s_y, b * NT + t - 3)
                    if t % TPC == 0:
                        pe.wait_ge(s_hlo, b * 16 + 8 * (c + 1))
                    for i in range(IT):
                        mm = three(banks[t % 4][:, 0:D], (hid_hi[c][:, i, toks], hid_lo[c][:, i, toks]),
                                   (down_hi[:, i, :], down_lo[:, i, :]), i == 0, i == IT - 1)
                    mm.then_inc(s_dn, 1)
                for kind, i in FIRST_ORDER:
                    if kind == "scores":
                        if i == 0:
                            pe.wait_ge(s_y, b * NT + NT)
                            pe.wait_ge(s_projlo, n0 * UNITS + 4)
                        if i >= 2:
                            pe.wait_ge(s_exp, n0 * TILES + i - 1)
                        scores(i)
                    elif kind == "proj":
                        if i in (0, 4, 8):
                            pe.wait_ge(s_wlo[i // 4], n0 + 2)
                        if i >= 4:
                            pe.wait_ge(s_projlo, n0 * UNITS + i - 3)
                        proj_products(banks[4 + i % 4], i)
                with pe.Fori(0, PAIRS - 1) as g:
                    step(b, b * PAIRS + g, False)
                step(b, b * PAIRS + PAIRS - 1, True)

        @block.scalar
        def _(act):
            def hi(dst, src, scale=1.0):
                return act.activation(dst, src, ACT.Copy, scale=scale)

            def weights_hi(n, part):
                act.wait_ge(s_raw[part], n * (32 if part <= PART_QK1 else 16) + (32 if part <= PART_QK1 else 16))
                hi(w_hi[:, part, :], w_raw[:, part, :]).then_inc(s_whi[part], 1)

            def proj_hi(ps, n, u):
                dst, _, is_q = proj_out(u)
                act.wait_ge(s_proj, n * UNITS + u + 1)
                hi(dst, ps, SCALE if is_q else 1.0).then_inc(s_projhi, 1)

            def exp(n, q):
                _, j, _, r, i = tile_of(q)
                w = (i + 1) * P
                act.wait_ge(s_max, n * TILES + q + 1)
                act.activation(prob[j][:, r, 0:w], ps_scores[q % 2][:, 0:w], ACT.Exp, bias=neg_max[:, q % TILES:q % TILES + 1],
                               accum_out=prob_sum[:, q % TILES:q % TILES + 1]).then_inc(s_exp, 1)

            def step(b, n, last):
                for kind, i, where in step_order(last):
                    if kind == "exp":
                        exp(n, i)
                    elif kind == "turn":
                        dst, _, at = turned(i)
                        act.wait_ge(s_pt, n * SLOTS + i + 1)
                        hi(dst, ps_turn[i % 2][:, at:CH]).then_inc(s_pthi, 1)
                    elif kind == "out":
                        act.wait_ge(s_pv, n * SLOTS + SLOT_BEGIN[i + 1])
                        hi(oT_hi[:, i // 2, (i % 2) * CH:(i % 2 + 1) * CH], ps_out[:, :]).then_inc(s_othi, 1)
                    elif kind == "weights":
                        if i == PART_O:
                            act.wait_ge(s_acc, n * WO_UNITS + 1)
                        weights_hi(n if i == PART_O else n + 1, i)
                    elif kind == "proj":
                        proj_hi(unit_banks[where], n + 1, i)
                    elif kind == "xturn":
                        x_hi(unit_banks[where], b + 1, i)

            def x_hi(ps, b, g):
                act.wait_ge(s_xt, b * 4 + g + 1)
                hi(xT_hi[:, g % 2, (g // 2) * CH:(g // 2 + 1) * CH], ps).then_inc(s_xthi, 1)

            act.wait_ge(s_out, 32)
            hi(eg_hi[:, :, :], eg_raw).then_inc(s_fhi, 1)
            act.wait_ge(s_upraw, 16)
            hi(up_hi[:, :, :], up_raw).then_inc(s_fhi, 1)
            for g in range(4):
                x_hi(banks[4 + g], 0, g)
            act.wait_ge(s_downraw, 16)
            hi(down_hi[:, :, :], down_raw).then_inc(s_fhi, 1)
            act.wait_ge(s_flo, 3)
            with act.Fori(0, B) as b:
                n0 = b * PAIRS
                def hidden_hi(e):
                    act.wait_ge(s_hid, b * 16 + e + 1)
                    hi(hid_hi[e // IT][:, e % IT, :], hid[:, e % IT, :]).then_inc(s_hhi, 1)

                for e in range(NC * IT):
                    if e >= IT:
                        act.wait_ge(s_hlo, b * 16 + e - IT + 1)
                    act.wait_ge(s_up, b * 16 + e + 1)
                    act.activation(hid[:, e % IT, :], banks[e % 4], ACT.Relu).then_inc(s_relu, 1)
                    if e > 0:
                        hidden_hi(e - 1)
                    if e >= NC * IT - 3:
                        weights_hi(n0, (PART_QK0, PART_QK1, PART_V)[e - NC * IT + 3])
                hidden_hi(NC * IT - 1)
                for kind, i in FIRST_ORDER:
                    if kind == "exp":
                        exp(n0, i)
                    elif kind == "proj":
                        proj_hi(banks[4 + i % 4], n0, i)
                with act.Fori(0, PAIRS - 1) as g:
                    step(b, b * PAIRS + g, False)
                step(b, b * PAIRS + PAIRS - 1, True)
                act.wait_ge(s_acc, b * PAIRS * WO_UNITS + PAIRS * WO_UNITS + 1)
                act.dma_start(out_v[b], acc[:, :, :]).then_inc(s_out, 16)
            act.wait_ge(s_out, 16 * B + 32)

        @block.vector
        def _(dve):
            def proj_lo(ps, n, u):
                h_, l_, is_q = proj_out(u)
                dve.wait_ge(s_projhi, n * UNITS + u + 1)
                if is_q:
                    ins = dve.scalar_tensor_tensor(out=l_, in0=ps, scalar=SCALE, in1=h_, op0=ALU.mult, op1=ALU.subtract)
                else:
                    ins = dve.tensor_tensor(l_, ps, h_, ALU.subtract)
                ins.then_inc(s_projlo, 1)

            def maximum(n, q):
                _, _, _, _, i = tile_of(q)
                diagonal = ps_scores[q % 2][:, i * P:(i + 1) * P]
                dve.wait_ge(s_sc, n * TILES + q + 1)
                dve.tensor_tensor(diagonal, diagonal, mask[:, :], ALU.add).then_inc(s_masked, 1)
                dve.wait_ge(s_masked, n * TILES + q + 1)
                dve.tensor_reduce(neg_max[:, q % TILES:q % TILES + 1], ps_scores[q % 2][:, 0:(i + 1) * P], AX.X, ALU.max,
                                  negate=True).then_inc(s_max, 1)

            def step(b, n, last):
                for kind, i, where in step_order(last):
                    if kind == "scores":
                        maximum(n, i)
                    elif kind == "turn":
                        h_, l_, at = turned(i)
                        dve.wait_ge(s_pthi, n * SLOTS + i + 1)
                        dve.tensor_tensor(l_, ps_turn[i % 2][:, at:CH], h_, ALU.subtract).then_inc(s_ptlo, 1)
                    elif kind == "out":
                        cols = slice((i % 2) * CH, (i % 2 + 1) * CH)
                        dve.wait_ge(s_othi, n * HALVES + i + 1)
                        dve.tensor_tensor(oT_lo[:, i // 2, cols], ps_out[:, :], oT_hi[:, i // 2, cols], ALU.subtract).then_inc(s_otlo, 1)
                        four = slice(4 * i, 4 * i + 4)
                        dve.reciprocal(prob_rcp[:, four], prob_sum[:, four]).then_inc(s_rcp, 1)
                    elif kind == "proj":
                        proj_lo(unit_banks[where], n + 1, i)
                    elif kind == "wo":
                        dve.wait_ge(s_rcp, n * HALVES + i // 2 + 1)
                        dve.wait_ge(s_acc, n * WO_UNITS + (1 if i < 4 else i - 2))
                        dve.wait_ge(s_wo, n * WO_UNITS + i + 1)
                        for a, t in enumerate(wo_tiles(i)):
                            q = 4 * (i // 2) + t % 4
                            last_add = dve.scalar_tensor_tensor(out=acc[:, t, :], in0=unit_banks[where][:, a * D:(a + 1) * D],
                                                                scalar=prob_rcp[:, q:q + 1], in1=acc[:, t, :], op0=ALU.mult, op1=ALU.add)
                        last_add.then_inc(s_acc, 1)
                    elif kind == "expert":
                        if i == 0:
                            dve.wait_ge(s_fin, b * NT + NT)
                        expert_read(unit_banks[where], b + 1, i)
                    elif kind == "xturn":
                        x_lo(unit_banks[where], b + 1, i)

            dve.memset(ps_out[:, 0:1], 0.0).then_inc(s_otlo, 1)
            dve.memset(ps_proj[:, 0:1], 0.0).then_inc(s_acc, 1)
            dve.memset(pD_hi[:, 0:P].bitcast(F32), 0.0).then_inc(s_dve, 1)
            dve.memset(pD_lo[:, 0:P].bitcast(F32), 0.0).then_inc(s_dve, 1)

            def statistics(stats, src, t):
                dve.bn_stats(stats[:, t, :], src[:, t, :])
                return dve.bn_stats(stats[:, t + 1, :], src[:, t + 1, :])

            def normed(half_of_tiles):
                for t in range(TPC * half_of_tiles, TPC * (half_of_tiles + 1)):
                    dve.tensor_scalar(xin[:, t, :], xin[:, t, :], mean_x[:, t:t + 1], rstd_x[:, t:t + 1],
                                      ALU.subtract, ALU.mult).then_inc(s_xn, 1)

            def x_lo(ps, b, g):
                dst = slice((g // 2) * CH, (g // 2 + 1) * CH)
                dve.wait_ge(s_xthi, b * 4 + g + 1)
                dve.tensor_tensor(xT_lo[:, g % 2, dst], ps, xT_hi[:, g % 2, dst], ALU.subtract).then_inc(s_xtlo, 1)

            def expert_read(ps, b, t):
                dve.wait_ge(s_eg, b * NT + t + 1)
                dve.tensor_copy(y[:, t, :], ps[:, 0:D])
                dve.max(top8[:, t, :], ps[:, D:GW]).then_inc(s_egread, 1)

            dve.wait_ge(s_const, 2)
            dve.wait_ge(s_xin, 16)
            for i in range(NT // 2):
                last = statistics(stats_x, xin, 2 * i)
            last.then_inc(s_stats, 1)
            def ffn_weights_lo(i, raw, h_, l_):
                dve.wait_ge(s_fhi, i + 1)
                dve.tensor_tensor(l_[:, :, :], raw, h_[:, :, :], ALU.subtract).then_inc(s_flo, 1)

            ffn_weights_lo(0, eg_raw, eg_hi, eg_lo)
            ffn_weights_lo(1, up_raw, up_hi, up_lo)
            dve.wait_ge(s_moments, 1)
            normed(0)
            normed(1)
            for g in range(4):
                x_lo(banks[4 + g], 0, g)
            for t in range(NT):
                expert_read(banks[t % 4], 0, t)
            ffn_weights_lo(2, down_raw, down_hi, down_lo)
            with dve.Fori(0, B) as b:
                n0 = b * PAIRS
                def feed_forward_sum(t):
                    dve.wait_ge(s_dn, b * NT + t + 1)
                    dve.scalar_tensor_tensor(out=y[:, t, :], in0=y[:, t, :], scalar=top2[:, t:t + 1], in1=banks[t % 4][:, 0:D],
                                             op0=ALU.mult, op1=ALU.add).then_inc(s_y, 1)

                def normed_y(c):
                    dve.wait_ge(s_moments, b * 3 + 3 + c)
                    for t in range(TPC * c, TPC * (c + 1)):
                        dve.tensor_scalar(y[:, t, :], y[:, t, :], mean[:, t:t + 1], rstd[:, t:t + 1],
                                          ALU.subtract, ALU.mult).then_inc(s_yn, 1)

                def hidden_lo(e):
                    dve.wait_ge(s_hhi, b * 16 + e + 1)
                    dve.tensor_tensor(hid_lo[e // IT][:, e % IT, :], hid[:, e % IT, :], hid_hi[e // IT][:, e % IT, :],
                                      ALU.subtract).then_inc(s_hlo, 1)

                for e in range(NC * IT):
                    dve.wait_ge(s_relu, b * 16 + e + 1)
                    r = hid[:, e % IT, :]
                    dve.tensor_tensor(r, r, r, ALU.mult).then_inc(s_hid, 1)
                    if e > 0:
                        hidden_lo(e - 1)
                hidden_lo(NC * IT - 1)
                dve.wait_ge(s_egread, b * NT + NT)
                dve.tensor_tensor(top2[:, :], top8[:, :, 0], top8[:, :, 1], ALU.add).then_inc(s_top2, 1)
                dve.wait_ge(s_top2, b + 1)
                dve.wait_ge(s_xin, b * 16 + 32)
                for t in range(NT):
                    feed_forward_sum(t)
                    if t == 0:
                        statistics(stats_x, xin, 0)
                        statistics(stats_x, xin, 2)
                    if t == 1:
                        statistics(stats_x, xin, 4)
                        statistics(stats_x, xin, 6).then_inc(s_stats, 1)
                    if t == TPC - 1 or t == NT - 1:
                        dve.wait_ge(s_y, b * NT + t + 1)
                    if t == TPC - 1:
                        statistics(stats, y, 0)
                        statistics(stats, y, 2).then_inc(s_stats, 1)
                    if t == 4:
                        dve.wait_ge(s_moments, b * 3 + 2)
                        normed(0)
                        normed(1)
                    if t == 6:
                        dve.wait_ge(s_y, b * NT + 6)
                        statistics(stats, y, 4)
                        normed_y(0)
                for kind, i in FIRST_ORDER:
                    if kind == "scores":
                        maximum(n0, i)
                    elif kind == "proj":
                        proj_lo(banks[4 + i % 4], n0, i)
                    elif kind == "stats":
                        ins = statistics(stats, y, 2 * i)
                        if i == NT // 2 - 1:
                            ins.then_inc(s_stats, 1)
                    elif kind == "normed":
                        normed_y(i)
                with dve.Fori(0, PAIRS - 1) as g:
                    step(b, b * PAIRS + g, False)
                step(b, b * PAIRS + PAIRS - 1, True)


_INS = ["L0_attn_hidden_states", "L0_attn_Wq", "L0_attn_Wk", "L0_attn_Wv", "L0_attn_Wo", "L0_ffn_gate_w",
        "L0_ffn_up_w", "L0_ffn_down_w", "L0_ffn_expert_weight", "L0_ffn_ln_gamma", "L0_ffn_ln_beta"]


def kernel(**inputs):
    import numpy as _np
    import concourse.bacc as _bacc
    from concourse import mybir as _mybir
    from concourse.bass_utils import run_bass_kernel_spmd as _run

    nc = _bacc.Bacc("TRN2", target_bir_lowering=False, num_devices=1)
    arrays, args = {}, []
    for name in _INS:
        a = _np.ascontiguousarray(inputs[name])
        arrays[f"in_{name}_dram"] = a
        args.append(nc.dram_tensor(f"in_{name}_dram", a.shape, _mybir.dt.from_np(a.dtype), kind="ExternalInput").ap())
    shape = inputs[_INS[0]].shape
    out = nc.dram_tensor("out_0_dram", shape, _mybir.dt.float32, kind="ExternalOutput").ap()
    layer_kernel(nc, *args, out)
    r = _run(nc, [arrays], core_ids=[0])
    return r.results[0]["out_0_dram"]
```
